# Optimizing a Trainium2 kernel written in Bass

```python
import numpy as np
import jax
import jax.numpy as jnp

def _softmax(x, axis=-1):
    return jax.nn.softmax(x, axis=axis)
def _gelu(x):
    return jax.nn.gelu(x, approximate=True)
def _silu(x):
    return jax.nn.silu(x)
def _sigmoid(x):
    return jax.nn.sigmoid(x)
def _layernorm(x, axis=-1, eps=1e-5):
    m = jnp.mean(x, axis=axis, keepdims=True)
    v = jnp.var(x, axis=axis, keepdims=True)
    return (x - m) / jnp.sqrt(v + eps)
def _scatter_add(tgt, idx, src, axis=0):
    return tgt.at[idx].add(src)
def _segment_sum(src, seg, n):
    return jax.ops.segment_sum(src, seg, n)

kernel_name = 'mk_conv_attn_hybrid_d2_conv_nchw128_4fc5e9'

def setup_inputs(seed: int = 0):
    np.random.seed(seed)
    _w = jnp.asarray
    def _rec_inputs():
        import jax
        import jax.numpy as jnp
        _gk = jax.random.key(seed)
        x = -0.0005207 + 1.001 * jax.random.normal(jax.random.fold_in(_gk, 1), (4, 128, 64, 64), jnp.float32)
        return x
    x = _rec_inputs()
    def _L0_conv_setup():
        import jax, jax.numpy as jnp
        import numpy as np

        def _prelu(x, a):
            return jnp.where(x >= 0, x, a * x)

        def _conv1x1(x, w, b, a):
            y = jnp.einsum('oc,nchw->nohw', w, x) + b[None, :, None, None]
            return _prelu(y, a)
        key = jax.random.key(seed)
        ks = jax.random.split(key, 8)
        N, C, H, W = (4, 128, 64, 64)
        Cr = C // 2
        sC = 1.0 / np.sqrt(C)
        x = jax.random.normal(ks[0], (N, C, H, W), dtype=jnp.float32)
        w1 = jax.random.normal(ks[1], (Cr, C), dtype=jnp.float32) * sC
        b1 = jnp.zeros((Cr,), dtype=jnp.float32)
        a1 = jnp.asarray(0.25, dtype=jnp.float32)
        w2 = jax.random.normal(ks[2], (Cr, C), dtype=jnp.float32) * sC
        b2 = jnp.zeros((Cr,), dtype=jnp.float32)
        a2 = jnp.asarray(0.25, dtype=jnp.float32)
        wa = jax.random.normal(ks[3], (C, C), dtype=jnp.float32) * sC
        ba = jnp.zeros((C,), dtype=jnp.float32)
        aa = jnp.asarray(0.25, dtype=jnp.float32)
        return {'x': x, 'w1': w1, 'b1': b1, 'a1': a1, 'w2': w2, 'b2': b2, 'a2': a2, 'wa': wa, 'ba': ba, 'aa': aa}
    _L0_conv_all = _L0_conv_setup()
    _L0_conv_in = {k: v for k, v in _L0_conv_all.items() if k in ('w1', 'b1', 'a1', 'w2', 'b2', 'a2', 'wa', 'ba', 'aa', )}
    del _L0_conv_all

    def _L1_attn_setup():
        import jax, jax.numpy as jnp
        import numpy as np
        SCALE_DIM = 128
        key = jax.random.key(seed)
        inputs = jax.random.normal(key, (16, 2048, 128), dtype=jnp.float32)
        return {'inputs': inputs}
    _L1_attn_all = _L1_attn_setup()
    _L1_attn_in = {k: v for k, v in _L1_attn_all.items() if k in ()}
    del _L1_attn_all

    def _L1_ffn_setup():
        import jax, jax.numpy as jnp
        import numpy as np
        BN_EPS = 1e-05
        key = jax.random.key(seed)
        k1, k2, k3 = jax.random.split(key, 3)
        B, T, I, H = (64, 2048, 128, 128)
        x = jax.random.normal(k1, (B, T, I), dtype=jnp.float32)
        W = jax.random.normal(k2, (H, I), dtype=jnp.float32) * (1.0 / np.sqrt(I))
        V = jnp.linalg.qr(jax.random.normal(k3, (H, H), dtype=jnp.float32))[0]
        gamma = jnp.ones((H,), dtype=jnp.float32)
        beta = jnp.zeros((H,), dtype=jnp.float32)
        return {'x': x, 'W': W, 'V': V, 'gamma': gamma, 'beta': beta}
    _L1_ffn_all = _L1_ffn_setup()
    _L1_ffn_in = {k: v for k, v in _L1_ffn_all.items() if k in ('W', 'V', 'gamma', 'beta', )}
    del _L1_ffn_all

    return {
        "x": x,
        "L0_conv_w1": _L0_conv_in["w1"],
        "L0_conv_b1": _L0_conv_in["b1"],
        "L0_conv_a1": _L0_conv_in["a1"],
        "L0_conv_w2": _L0_conv_in["w2"],
        "L0_conv_b2": _L0_conv_in["b2"],
        "L0_conv_a2": _L0_conv_in["a2"],
        "L0_conv_wa": _L0_conv_in["wa"],
        "L0_conv_ba": _L0_conv_in["ba"],
        "L0_conv_aa": _L0_conv_in["aa"],
        "L1_ffn_W": _L1_ffn_in["W"],
        "L1_ffn_V": _L1_ffn_in["V"],
        "L1_ffn_gamma": _L1_ffn_in["gamma"],
        "L1_ffn_beta": _L1_ffn_in["beta"],
    }

def reference(x, L0_conv_w1, L0_conv_b1, L0_conv_a1, L0_conv_w2, L0_conv_b2, L0_conv_a2, L0_conv_wa, L0_conv_ba, L0_conv_aa, L1_ffn_W, L1_ffn_V, L1_ffn_gamma, L1_ffn_beta):
    import jax
    import jax.numpy as jnp
    def _L0_conv_ref(x, w1, b1, a1, w2, b2, a2, wa, ba, aa):
        import jax, jax.numpy as jnp
        import numpy as np

        def _prelu(x, a):
            return jnp.where(x >= 0, x, a * x)

        def _conv1x1(x, w, b, a):
            y = jnp.einsum('oc,nchw->nohw', w, x) + b[None, :, None, None]
            return _prelu(y, a)
        N, C, H, W = x.shape
        HW = H * W
        e1 = _conv1x1(x, w1, b1, a1).reshape(N, -1, HW)
        e2 = _conv1x1(x, w2, b2, a2).reshape(N, -1, HW)
        asm = _conv1x1(x, wa, ba, aa).reshape(N, C, HW)
        score = jnp.einsum('nci,ncj->nij', e1, e2)
        score = jax.nn.softmax(score, axis=2)
        out = jnp.einsum('nij,ncj->nci', score, asm)
        return out.reshape(N, C, H, W)

    def _L1_attn_ref(inputs):
        import jax, jax.numpy as jnp
        import numpy as np
        SCALE_DIM = 128
        scores = jnp.einsum('bsd,btd->bst', inputs, inputs) / jnp.sqrt(jnp.asarray(inputs.shape[-1], inputs.dtype))
        att = jax.nn.softmax(scores, axis=-1)
        return jnp.einsum('bst,btd->bsd', att, inputs)

    def _L1_ffn_ref(x, W, V, gamma, beta):
        import jax, jax.numpy as jnp
        import numpy as np
        BN_EPS = 1e-05
        B, T, H = (x.shape[0], x.shape[1], W.shape[0])
        Wx = jnp.einsum('bti,hi->bth', x, W)
        flat = Wx.reshape(B * T, H)
        mean = jnp.mean(flat, axis=0)
        var = jnp.var(flat, axis=0)
        Wx = ((flat - mean) * jax.lax.rsqrt(var + BN_EPS) * gamma + beta).reshape(B, T, H)
        Vt = V.T

        def step(yt, wx_t):
            yt = jax.nn.sigmoid(wx_t + yt @ Vt)
            return (yt, yt)
        y0 = jnp.zeros((B, H), dtype=Wx.dtype)
        _, ys = jax.lax.scan(step, y0, jnp.swapaxes(Wx, 0, 1))
        return jnp.swapaxes(ys, 0, 1)

    def _gn(v, G=32, eps=1e-5):
        B_, C_, H_, W_ = v.shape
        g = v.reshape(B_, G, C_ // G, H_, W_)
        m = jnp.mean(g, axis=(2, 3, 4), keepdims=True)
        s = jnp.var(g, axis=(2, 3, 4), keepdims=True)
        return ((g - m) / jnp.sqrt(s + eps)).reshape(v.shape)

    def _ln_c(v, eps=1e-6):
        m = jnp.mean(v, axis=1, keepdims=True)
        s = jnp.var(v, axis=1, keepdims=True)
        return (v - m) / jnp.sqrt(s + eps)

    def _ln_t(v, eps=1e-5):
        m = jnp.mean(v, axis=-1, keepdims=True)
        s = jnp.var(v, axis=-1, keepdims=True)
        return (v - m) / jnp.sqrt(s + eps)

    def _to_tokens(v):
        B_, C_, H_, W_ = v.shape
        return v.reshape(B_, C_, H_ * W_).transpose(0, 2, 1)
    def _from_tokens(t, like):
        B_, C_, H_, W_ = like.shape
        return t.transpose(0, 2, 1).reshape(B_, C_, H_, W_)

    x = x + _L0_conv_ref(_gn(x), L0_conv_w1, L0_conv_b1, L0_conv_a1, L0_conv_w2, L0_conv_b2, L0_conv_a2, L0_conv_wa, L0_conv_ba, L0_conv_aa)
    t = _to_tokens(x)
    t = t + _L1_attn_ref(_ln_t(t))
    t = t + _L1_ffn_ref(_ln_t(t), L1_ffn_W, L1_ffn_V, L1_ffn_gamma, L1_ffn_beta)
    x = _from_tokens(t, x)
    return x


_drawn_inputs = setup_inputs


def setup_inputs(seed=0):
    import zlib

    import numpy as np

    out = dict(_drawn_inputs(seed))
    spreads = {'L0_conv_b1': (0.0, 0.1),
     'L0_conv_b2': (0.0, 0.1),
     'L0_conv_ba': (0.0, 0.1),
     'L1_ffn_gamma': (1.0, 0.6),
     'L1_ffn_beta': (0.0, 0.8)}
    factors = {}
    for name, (base, spread) in spreads.items():
        noise = np.random.default_rng([zlib.crc32(name.encode()), seed]).standard_normal(out[name].shape)
        drawn = base * np.exp(spread * noise) if base else spread * noise
        out[name] = jnp.asarray(drawn.astype(out[name].dtype))
    for name, factor in factors.items():
        out[name] = (out[name] * factor).astype(out[name].dtype)
    return out
```

```python
import concourse.bass as bass
from concourse import mybir
from contextlib import ExitStack
from math import log

F32 = mybir.dt.float32
F16 = mybir.dt.float16
I32 = mybir.dt.int32
ACT = mybir.ActivationFunctionType
ALU = mybir.AluOpType
AX = mybir.AxisListType


def hybrid_kernel(nc, x, w1, b1, a1, w2, b2, a2, wa, ba, aa, W, V, gamma, beta, out):
    B, C, T = x.shape
    CH = w1.shape[0]
    BLK = 512
    NB = T // BLK
    NP = T // 256
    GROUP = C // 32
    HALF = BLK // 2
    LIFT = 6.0 * log(2.0)
    MROW = 64.0
    ROWMAX = float(C) ** 0.5
    LEN = 32
    CHUNKS = T // LEN
    WARM = 12
    COLS = B * CHUNKS
    NG = 2
    GC = COLS // NG
    GB = B // NG
    CLOSE = 2.0 ** -18
    assert C == 128 and CH == 64 and T == 4096 and B == 4 and COLS == 512

    with ExitStack() as ctx:
        def sb(name, shape, dt=F32):
            return ctx.enter_context(nc.sbuf_tensor(name, shape, dt))

        def signal(name):
            return ctx.enter_context(nc.semaphore(name))

        X = sb("X", [C, B * T])
        REG = sb("REG", [C, 32768])

        def f32(at, n):
            return REG[:, at:at + n]

        def f16(at, n):
            return REG[:, at:at + n // 2].bitcast(F16)

        SET = 12288
        key_a = [f16(s * SET, T) for s in range(2)]
        key_b = [f16(s * SET + 2048, T) for s in range(2)]
        query_a = [f16(s * SET + 4096, T) for s in range(2)]
        query_b = [f16(s * SET + 6144, T) for s in range(2)]
        value_hi = [f16(s * SET + 8192, T) for s in range(2)]
        value_lo = [f16(s * SET + 10240, T) for s in range(2)]
        u_hi, u_lo, t_hi, t_lo = key_a, key_b, value_hi, value_lo
        WORK = 2 * SET
        p_hi = [f16(WORK + 512 * j, 1024) for j in range(4)]
        p_lo = [f16(WORK + 2048 + 512 * j, 1024) for j in range(4)]
        p_full = [f32(WORK + 4096 + 1024 * j, 1024) for j in range(2)]
        sum_run, sum_end, o_copy, o_norm = [f32(WORK + 6144 + 512 * j, BLK) for j in range(4)]
        g_buf = [f32(WORK + 512 * j, BLK) for j in range(2)]
        pos = [f32(WORK + 1024 + 512 * j, BLK) for j in range(3)]
        neg = [f32(WORK + 2560 + 512 * j, BLK) for j in range(3)]
        act_buf = [f32(WORK + 4096 + 512 * j, BLK) for j in range(3)]
        hi_tmp = f16(WORK + 5632, BLK)
        centered = f32(WORK, T)
        squares = [f32(WORK + 4096 + 512 * j, BLK) for j in range(2)]
        normed = [f32(WORK + 5120 + 512 * j, BLK) for j in range(2)]
        rstd_rows = REG[0:4, WORK + 6144:WORK + 7168]
        wx = f32(0, B * T)
        ys = f32(B * T, B * T).rearrange("p (s c) -> p s c", c=COLS)

        w_in = sb("w_in", [C, 5, C])
        w_t = sb("w_t", [C, 5, C])
        w1_t, w2_t, wa_t, W_t, V_t = [w_t[:, j, :] for j in range(5)]
        ident = sb("ident", [C, C])
        ident16 = sb("ident16", [C, C], F16)
        group_mean = sb("group_mean", [C, C])
        channel_mean = sb("channel_mean", [C, C])
        select = sb("select", [4, 4, C])
        ones = sb("ones", [C, C])
        ba_row = sb("ba_row", [1, C])
        a_row = sb("a_row", [1, 4])
        bias12 = sb("bias12", [C, 2])
        neg_bias = sb("neg_bias", [C, 2])
        neg_a = sb("neg_a", [C, 4])
        eps_gn = sb("eps_gn", [C, 1])
        lift = sb("lift", [C, 2])
        gb = sb("gb", [C, 2])
        gn_stats = sb("gn_stats", [C, B, NB, 6])
        gn_mv = sb("gn_mv", [C, B, 2])
        gn_ms = sb("gn_ms", [C, 2, B])
        gn_w = sb("gn_w", [C, 4, B])
        part_max = sb("part_max", [C, 128])
        tile_max = sb("tile_max", [C, T // 128])
        m_hi = sb("m_hi", [T // 128, 128], F16)
        m_lo = sb("m_lo", [T // 128, 128], F16)
        inv_sum = sb("inv_sum", [C, 4])
        inv_rows = sb("inv_rows", [4, C])
        ln_std = sb("ln_std", [C, T // 128])
        ln_rstd = sb("ln_rstd", [C, T // 128])
        bn_st = sb("bn_st", [C, B * NB, 6])
        bn_mv = sb("bn_mv", [C, 8])
        y_began = sb("y_began", [C, COLS])
        z_buf = w_in[:, 0:COLS // C, :].rearrange("p j c -> p (j c)")
        gap = sb("gap", [C, 4])
        flag = sb("flag", [1, 1], I32)

        PS = ctx.enter_context(nc.psum_tensor("PS", [C, 8 * BLK], F32))

        def bank(j, n=1):
            return PS[:, j * BLK:(j + n) * BLK]

        o_bank, mx_bank, small_bank = bank(4), bank(5, 2), bank(7)

        x_loaded = [signal(f"x_loaded{b}") for b in range(B)]
        w_loaded = signal("w_loaded")
        consts_set = signal("consts_set")
        w_turned = signal("w_turned")
        w_ready = signal("w_ready")
        alpha_ready = signal("alpha_ready")
        dve_step = signal("dve_step")
        pool_step = signal("pool_step")
        gn_sums = signal("gn_sums")
        gn_mean = signal("gn_mean")
        gn_std = signal("gn_std")
        g_ready = signal("g_ready")
        proj_done = signal("proj_done")
        relu_done = signal("relu_done")
        act_done = signal("act_done")
        hi_copied = signal("hi_copied")
        lo_made = signal("lo_made")
        split_done = signal("split_done")
        mx_ready = signal("mx_ready")
        mx_read = signal("mx_read")
        max_found = signal("max_found")
        max_turned = signal("max_turned")
        m_ready = signal("m_ready")
        m_moved = signal("m_moved")
        scores_ready = signal("scores_ready")
        hi_ready = signal("hi_ready")
        full_ready = signal("full_ready")
        lo_ready = signal("lo_ready")
        pv_done = signal("pv_done")
        sum_half = signal("sum_half")
        sum_added = signal("sum_added")
        o_copied = signal("o_copied")
        sums_ready = signal("sums_ready")
        inv_ready = signal("inv_ready")
        inv_turned = signal("inv_turned")
        rows_ready = signal("rows_ready")
        inv_spread = signal("inv_spread")
        o_normed = signal("o_normed")
        x_updated = signal("x_updated")
        mean_ready = signal("mean_ready")
        xc_ready = signal("xc_ready")
        sq_ready = signal("sq_ready")
        var_ready = signal("var_ready")
        std_ready = signal("std_ready")
        rstd_ready = signal("rstd_ready")
        rstd_turned = signal("rstd_turned")
        rrows_ready = signal("rrows_ready")
        rstd_spread = signal("rstd_spread")
        u_ready = signal("u_ready")
        uhi_ready = signal("uhi_ready")
        ulo_ready = signal("ulo_ready")
        u_turned = signal("u_turned")
        t_copied = signal("t_copied")
        wx_ready = signal("wx_ready")
        wx_stored = signal("wx_stored")
        wx_counted = signal("wx_counted")
        bn_std = signal("bn_std")
        bn_var = signal("bn_var")
        bn_ready = signal("bn_ready")
        vy_ready = [signal(f"vy_ready{g}") for g in range(NG)]
        z_ready = [signal(f"z_ready{g}") for g in range(NG)]
        y_ready = [signal(f"y_ready{g}") for g in range(NG)]
        start_set = signal("start_set")
        gap_ready = signal("gap_ready")
        gap_max = signal("gap_max")
        flag_ready = signal("flag_ready")
        out_ready = signal("out_ready")
        stored = signal("stored")

        block = ctx.enter_context(nc.Block())
        x_v = x.rearrange("b c t -> c b t")
        out_v = out.rearrange("b c t -> c b t")

        def cols(b, q):
            return bass.ds(b * T + q * BLK, BLK)

        def blk(q):
            return bass.ds(q * BLK, BLK)

        wx_steps = wx.rearrange("p (n s) -> p n s", s=LEN)
        SEQ = CHUNKS - 1

        def state(s):
            if s >= WARM:
                return ys[:, s - WARM, :]
            return y_began[:, :] if s == WARM - 1 else ys[:, LEN // 2 + s % 2, :]

        def seq_cols(buf, s, k):
            return buf[:, s, :].rearrange("p (b k) -> p b k", b=B)[:, :, bass.ds(k, 1)]

        @block.sync
        def _(sp):
            for b in range(B):
                sp.dma_start(X[:, b * T:(b + 1) * T], x[b]).then_inc(x_loaded[b], 16)
                if b == 0:
                    for half in range(2):
                        rows = slice(CH * half, CH * half + CH)
                        sp.dma_start(w_in[rows, 0, :], w1).then_inc(w_loaded, 16)
                        sp.dma_start(w_in[rows, 1, :], w2).then_inc(w_loaded, 16)
                        sp.dma_start(bias12[rows, 0:1], b1).then_inc(w_loaded, 16)
                        sp.dma_start(bias12[rows, 1:2], b2).then_inc(w_loaded, 16)
                    for j, w in enumerate((wa, W, V)):
                        sp.dma_start(w_in[:, 2 + j, :], w).then_inc(w_loaded, 16)
                    sp.dma_start(gb[:, 0:1], gamma).then_inc(w_loaded, 16)
                    sp.dma_start(gb[:, 1:2], beta).then_inc(w_loaded, 16)
                    sp.dma_start(ba_row[:, :], ba).then_inc(w_loaded, 16)
                    for j, a in enumerate((a1, a2, aa)):
                        sp.dma_start(a_row[0:1, j:j + 1], a).then_inc(w_loaded, 16)
            for b in range(B):
                sp.wait_ge(m_ready, b + 1)
                for row, part in ((CH, m_hi), (CH + 1, m_lo)):
                    sp.dma_start(query_b[b % 2][row:row + 1, :].rearrange("o (t p) -> o t p", p=128),
                                 part[:, :]).then_inc(m_moved, 16)
            for b in range(B):
                sp.wait_ge(out_ready, b + 1)
                sp.dma_start(out[b], X[:, b * T:(b + 1) * T]).then_inc(stored, 16)
            sp.wait_ge(stored, 16 * B)

        W_LOADS = 16 * (8 + 3 + 3 + 3)

        @block.tensor
        def _(pe):
            pe.sem_inc(proj_done, 1)
            pe.sem_inc(pv_done, 3)
            pe.sem_inc(var_ready, 1)
            pe.sem_inc(wx_ready, 1)

            pe.wait_ge(w_loaded, W_LOADS)
            pe.wait_ge(consts_set, 1)
            for j in range(5):
                last = nc.tensor.transpose(PS[:, j * C:(j + 1) * C], w_in[:, j, :], ident[:, :])
            last.then_inc(w_turned, 1)
            nc.tensor.matmul(small_bank[:, 0:3], ones[0:1, :], a_row[0:1, 0:3], start=True, stop=True) \
                .then_inc(w_turned, 1)
            pe.wait_ge(gn_sums, 1)
            pe.wait_ge(alpha_ready, 1)
            nc.tensor.matmul(small_bank[:, 0:2 * B], group_mean[:, :], gn_ms[:, :, :].rearrange("p k b -> p (k b)"),
                             start=True, stop=True).then_inc(gn_mean, 1)
            pe.wait_ge(w_ready, 1)

            def prepare(b):
                with pe.Fori(0, NB // 2) as i:
                    for h in range(2):
                        n = b * NB + 2 * i + h
                        pe.wait_ge(g_ready, n + 1)
                        pe.wait_ge(relu_done, n)
                        g = g_buf[h]
                        nc.tensor.matmul(bank(3 * h), w1_t, g, start=True, stop=True)
                        nc.tensor.matmul(bank(3 * h + 1), w2_t, g, start=True, stop=True)
                        for t in range(4):
                            o = bank(3 * h + 2)[:, t * C:(t + 1) * C]
                            nc.tensor.matmul(o, g[:, t * 128:(t + 1) * 128], wa_t, start=True, stop=False)
                            last = nc.tensor.matmul(o, ones[0:1, :], ba_row[0:1, :], start=False, stop=True)
                        last.then_inc(proj_done, 1)

            def max_scores(b, ib, p):
                v = b * 128 + ib * 16 + p
                pe.wait_ge(mx_read, v)
                for t in range(2):
                    last = nc.tensor.matmul(mx_bank[:, t * BLK:(t + 1) * BLK],
                                            query_a[b % 2][:, bass.ds(ib * BLK + p // 4 * 128, 128)],
                                            key_a[b % 2][:, (p % 4 * 2 + t) * BLK:(p % 4 * 2 + t + 1) * BLK],
                                            start=True, stop=True)
                last.then_inc(mx_ready, 1)

            def turn_max(b):
                pe.wait_ge(max_found, b + 1)
                nc.tensor.transpose(small_bank[0:T // 128, 0:128], tile_max[:, :], ident[:, :]) \
                    .then_inc(max_turned, 1)

            def products(m):
                s = m % 2
                if m < B:
                    return [(key_a[s], query_a[s], C), (key_b[s], query_b[s], CH + 2)], value_hi[s], value_lo[s]
                return [(u_hi[s], u_hi[s], C), (u_hi[s], u_lo[s], C), (u_lo[s], u_hi[s], C)], t_hi[s], t_lo[s]

            def attend(m):
                score_terms, v_hi, v_lo = products(m)
                mx = m + 1 < B

                def scores(ib, p):
                    n = m * 128 + ib * 16 + p
                    pe.wait_ge(full_ready, n)
                    for t in range(2):
                        j = 2 * p + t
                        for k, (key, query, rows) in enumerate(score_terms):
                            last = nc.tensor.matmul(bank(p % 2 * 2 + t), key[0:rows, j * 128:(j + 1) * 128],
                                                    query[0:rows, blk(ib)], start=(k == 0),
                                                    stop=(k == len(score_terms) - 1))
                    last.then_inc(scores_ready, 1)

                def weigh(ib, p):
                    n = m * 128 + ib * 16 + p
                    pe.wait_ge(lo_ready, n + 2)
                    if p == 0:
                        pe.wait_ge(o_copied, m * NB + ib)
                    for t in range(2):
                        j = 2 * p + t
                        terms = ((v_hi, p_hi), (v_lo, p_hi), (v_hi, p_lo))
                        for k, (v, e) in enumerate(terms):
                            last = nc.tensor.matmul(o_bank, v[:, j * 128:(j + 1) * 128],
                                                    e[p % 4][:, t * BLK:(t + 1) * BLK],
                                                    start=(p == 0 and t == 0 and k == 0),
                                                    stop=(p == NP - 1 and t == 1 and k == 2))
                    last.then_inc(pv_done, 1)

                def column_sums(ib):
                    nb = m * NB + ib
                    pe.wait_ge(sum_added, (nb + 1) * 16 + 1)
                    pe.wait_ge(o_normed, nb + 1)
                    for t in range(4):
                        last = nc.tensor.matmul(small_bank[:, t:t + 1], sum_end[:, t * 128:(t + 1) * 128],
                                                ones[:, 0:1], start=True, stop=True)
                    last.then_inc(sums_ready, 1)

                def turn_inverse(ib):
                    pe.wait_ge(inv_ready, m * NB + ib + 1)
                    nc.tensor.transpose(small_bank[0:4, 0:128], inv_sum[:, :], ident[:, :]) \
                        .then_inc(inv_turned, 1)

                def spread_inverse(ib):
                    pe.wait_ge(rows_ready, m * NB + ib + 1)
                    for t in range(4):
                        last = nc.tensor.matmul(small_bank[:, t * 128:(t + 1) * 128], select[0:4, t, :],
                                                inv_rows[:, :], start=True, stop=True)
                    last.then_inc(inv_spread, 1)

                def body(ib, first):
                    for p in range(NP):
                        scores(ib, p)
                        if mx:
                            max_scores(m + 1, ib, p)
                        if p >= 2:
                            weigh(ib, p - 2)
                        elif not first:
                            weigh(ib - 1, NP + p - 2)
                        if not first:
                            if p == 5:
                                column_sums(ib - 1)
                            if p == 7:
                                turn_inverse(ib - 1)
                            if p == 9:
                                spread_inverse(ib - 1)

                body(0, True)
                with pe.Fori(1, NB) as ib:
                    body(ib, False)
                weigh(NB - 1, NP - 2)
                weigh(NB - 1, NP - 1)
                column_sums(NB - 1)
                turn_inverse(NB - 1)
                spread_inverse(NB - 1)

            def channel_norm(k):
                b = k % B
                with pe.Fori(0, NB // 2) as i:
                    for h in range(2):
                        n = k * NB + 2 * i + h
                        pe.wait_ge(xc_ready, n)
                        nc.tensor.matmul(bank(h), channel_mean[:, :], X[:, cols(b, 2 * i + h)],
                                         start=True, stop=True).then_inc(mean_ready, 1)
                    for h in range(2):
                        n = k * NB + 2 * i + h
                        pe.wait_ge(sq_ready, n + 1)
                        for t in range(4):
                            last = nc.tensor.matmul(bank(2)[:, bass.ds(8 * i + 4 * h + t, 1)],
                                                    squares[h][:, t * 128:(t + 1) * 128],
                                                    channel_mean[:, 0:1], start=True, stop=True)
                        last.then_inc(var_ready, 1)
                pe.wait_ge(rstd_ready, k + 1)
                for q in range(NB):
                    last = nc.tensor.transpose(PS[0:4, 3 * BLK + q * 128:3 * BLK + (q + 1) * 128],
                                               ln_rstd[:, 4 * q:4 * q + 4], ident[:, :])
                last.then_inc(rstd_turned, 1)
                pe.wait_ge(rrows_ready, k + 1)
                with pe.Fori(0, NB // 2) as i:
                    for h in range(2):
                        n = k * NB + 2 * i + h
                        pe.wait_ge(u_ready, n)
                        for t in range(4):
                            last = nc.tensor.matmul(bank(h)[:, t * 128:(t + 1) * 128], select[0:4, t, :],
                                                    rstd_rows[:, bass.ds((2 * i + h) * 128, 128)],
                                                    start=True, stop=True)
                        last.then_inc(rstd_spread, 1)
                    for h in range(2):
                        n = k * NB + 2 * i + h
                        if k < B:
                            pe.wait_ge(ulo_ready, n + 2)
                            pe.wait_ge(t_copied, n)
                            turned = bank(5 + h).bitcast(F16)
                            for part, src in enumerate((u_hi, u_lo)):
                                for t in range(4):
                                    last = nc.tensor.transpose(
                                        turned[:, part * BLK + t * 128:part * BLK + (t + 1) * 128],
                                        src[b % 2][:, bass.ds((2 * i + h) * BLK + t * 128, 128)], ident16[:, :])
                            last.then_inc(u_turned, 1)
                        else:
                            j = n - B * NB
                            pe.wait_ge(u_ready, n + 2)
                            pe.wait_ge(wx_stored, j)
                            nc.tensor.matmul(bank(5 + h), W_t, normed[h], start=True, stop=True) \
                                .then_inc(wx_ready, 1)

            prepare(0)
            pe.wait_ge(split_done, NB)
            with pe.Fori(0, NB) as ib:
                for p in range(16):
                    max_scores(0, ib, p)
            turn_max(0)
            for m in range(B):
                if m + 1 < B:
                    prepare(m + 1)
                    pe.wait_ge(split_done, (m + 2) * NB)
                pe.wait_ge(m_moved, 32 * (m + 1))
                attend(m)
                if m + 1 < B:
                    turn_max(m + 1)
            for m in range(B, 2 * B):
                pe.wait_ge(x_updated, m * NB)
                channel_norm(m - B)
                pe.wait_ge(t_copied, (m - B + 1) * NB + 1)
                attend(m)
            pe.wait_ge(x_updated, 2 * B * NB)
            for k in range(B, 2 * B):
                channel_norm(k)

            pe.wait_ge(bn_ready, 1)
            for s in range(1, WARM + LEN):
                for g in range(NG):
                    gs = slice(g * GC, (g + 1) * GC)
                    prev = state(s - 1)[:, gs]
                    pe.wait_ge(y_ready[g], s)
                    if s == WARM:
                        pe.wait_ge(start_set, 1)
                    nc.tensor.matmul(bank(g)[:, 0:GC], V_t, prev, start=True, stop=True) \
                        .then_inc(vy_ready[g], 1)
            pe.wait_ge(gap_ready, 1)
            nc.tensor.transpose(small_bank[0:1, 0:128], gap[:, 0:1], ident[:, :]).then_inc(gap_max, 1)
            pe.wait_ge(flag_ready, 1)
            far = pe.value_load(flag[0:1, 0:1], min_val=0, max_val=1)
            DONE = WARM + LEN
            with pe.If(far > 0):
                with pe.Fori(0, SEQ) as k:
                    for s in range(LEN):
                        prev = seq_cols(ys, (s - 1) % LEN, k + (1 if s else 0))
                        pe.wait_ge(y_ready[0], DONE + k * LEN + s)
                        nc.tensor.matmul(bank(0)[:, 0:B], V_t, prev, start=True, stop=True) \
                            .then_inc(vy_ready[0], 1)

        @block.scalar
        def _(act):
            act.sem_inc(relu_done, 1)
            act.sem_inc(full_ready, 1)
            act.sem_inc(uhi_ready, 1)
            act.sem_inc(t_copied, 1)
            act.sem_inc(wx_stored, 1)
            act.wait_ge(w_turned, 1)
            nc.scalar.activation(w_t[:, :, :].rearrange("p j c -> p (j c)"), PS[:, 0:5 * C], ACT.Copy) \
                .then_inc(w_ready, 1)
            act.wait_ge(w_turned, 2)
            nc.scalar.activation(neg_a[:, 0:3], small_bank[:, 0:3], ACT.Copy, scale=-1.0) \
                .then_inc(alpha_ready, 1)
            nc.scalar.activation(neg_bias[:, :], bias12[:, :], ACT.Copy, scale=-1.0) \
                .then_inc(alpha_ready, 1)
            act.wait_ge(gn_sums, 2)
            nc.scalar.activation(gn_w[:, 1, :], gn_w[:, 0, :], ACT.Sqrt, bias=eps_gn[:, 0:1]) \
                .then_inc(gn_std, 1)
            act.wait_ge(alpha_ready, 2)

            def prepare(b):
                with act.Fori(0, NB // 2) as i:
                    for h in range(2):
                        n = b * NB + 2 * i + h
                        act.wait_ge(proj_done, n + 2)
                        act.wait_ge(act_done, n)
                        for j in range(3):
                            src = bank(3 * h + j)
                            plus = bias12[:, j:j + 1] if j < 2 else 0.0
                            minus = neg_bias[:, j:j + 1] if j < 2 else 0.0
                            nc.scalar.activation(pos[j], src, ACT.Relu, bias=plus)
                            last = nc.scalar.activation(neg[j], src, ACT.Relu, bias=minus, scale=-1.0)
                        last.then_inc(relu_done, 1)

            def attend(m):
                scale = 1.0 if m < B else C ** -0.5
                bias = lift[:, 0:1] if m < B else lift[:, 1:2]

                def body(ib, first):
                    for p in range(NP):
                        n = m * 128 + ib * 16 + p
                        src = bank(p % 2 * 2, 2)
                        act.wait_ge(scores_ready, n + 1)
                        act.wait_ge(pv_done, n)
                        nc.scalar.activation(p_hi[p % 4], src, ACT.Exp, bias=bias, scale=scale) \
                            .then_inc(hi_ready, 1)
                        act.wait_ge(lo_ready, n)
                        act.wait_ge(sum_added, n)
                        nc.scalar.activation(p_full[p % 2], src, ACT.Exp, bias=bias, scale=scale) \
                            .then_inc(full_ready, 1)
                        if p == 1 and not first:
                            copy_out(ib - 1)

                def copy_out(ib):
                    nb = m * NB + ib
                    act.wait_ge(pv_done, (nb + 1) * 16 + 3)
                    act.wait_ge(o_normed, nb + 1)
                    nc.scalar.activation(o_copy, o_bank, ACT.Copy).then_inc(o_copied, 1)

                body(0, True)
                with act.Fori(1, NB) as ib:
                    body(ib, False)
                copy_out(NB - 1)

            def channel_norm(k):
                b = k % B
                with act.Fori(0, NB // 2) as i:
                    for h in range(2):
                        n = k * NB + 2 * i + h
                        act.wait_ge(xc_ready, n + 2)
                        act.wait_ge(var_ready, n)
                        nc.scalar.activation(squares[h], centered[:, blk(2 * i + h)], ACT.Square) \
                            .then_inc(sq_ready, 1)
                act.wait_ge(var_ready, (k + 1) * NB + 1)
                nc.scalar.activation(ln_std[:, :], bank(2)[:, 0:T // 128], ACT.Sqrt, bias=eps_gn[:, 0:1]) \
                    .then_inc(std_ready, 1)
                with act.Fori(0, NB // 2) as i:
                    if k < B:
                        for h in range(2):
                            n = k * NB + 2 * i + h
                            act.wait_ge(u_ready, n + 2)
                            nc.scalar.activation(u_hi[b % 2][:, blk(2 * i + h)], normed[h], ACT.Copy) \
                                .then_inc(uhi_ready, 1)
                        for h in range(2):
                            n = k * NB + 2 * i + h
                            act.wait_ge(u_turned, n + 1)
                            turned = bank(5 + h).bitcast(F16)
                            nc.scalar.activation(t_hi[b % 2][:, blk(2 * i + h)], turned[:, 0:BLK], ACT.Copy)
                            nc.scalar.activation(t_lo[b % 2][:, blk(2 * i + h)], turned[:, BLK:2 * BLK], ACT.Copy) \
                                .then_inc(t_copied, 1)
                    else:
                        for h in range(2):
                            n = (k - B) * NB + 2 * i + h
                            act.wait_ge(wx_ready, n + 2)
                            nc.scalar.activation(wx[:, cols(b, 2 * i + h)], bank(5 + h), ACT.Copy) \
                                .then_inc(wx_stored, 1)

            prepare(0)
            for m in range(B):
                if m + 1 < B:
                    prepare(m + 1)
                attend(m)
            for m in range(B, 2 * B):
                channel_norm(m - B)
                attend(m)
            for k in range(B, 2 * B):
                channel_norm(k)
            act.wait_ge(bn_var, 1)
            nc.scalar.activation(bn_mv[:, 2:3], bn_mv[:, 1:2], ACT.Sqrt, bias=eps_gn[:, 0:1]) \
                .then_inc(bn_std, 1)
            act.wait_ge(bn_ready, 1)
            shift = bn_mv[:, 5:6]
            for s in range(WARM + LEN):
                for g in range(NG):
                    gs = slice(g * GC, (g + 1) * GC)
                    dst = state(s)[:, gs]
                    act.wait_ge(z_ready[g], s + 1)
                    nc.scalar.activation(dst, z_buf[:, gs], ACT.Sigmoid, bias=shift).then_inc(y_ready[g], 1)
            act.wait_ge(flag_ready, 1)
            far = act.value_load(flag[0:1, 0:1], min_val=0, max_val=1)
            DONE = WARM + LEN
            with act.If(far > 0):
                with act.Fori(0, SEQ) as k:
                    for s in range(LEN):
                        act.wait_ge(z_ready[0], DONE + k * LEN + s + 1)
                        nc.scalar.activation(seq_cols(ys, s, k + 1), z_buf[:, 0:B].rearrange("p (b o) -> p b o", o=1),
                                             ACT.Sigmoid, bias=shift).then_inc(y_ready[0], 1)

        @block.vector
        def _(dve):
            dve.sem_inc(lo_ready, 1)
            dve.sem_inc(o_normed, 1)
            dve.sem_inc(xc_ready, 1)
            dve.sem_inc(u_ready, 1)
            dve.sem_inc(ulo_ready, 1)
            dve.sem_inc(wx_counted, 1)
            steps = [0]

            def link(ins):
                ins.then_inc(dve_step, 1)
                steps[0] += 1
                dve.wait_ge(dve_step, steps[0])

            for b in range(B):
                dve.wait_ge(x_loaded[b], 16)
                for q in range(NB):
                    last = nc.vector.bn_stats(gn_stats[:, b, q, :], X[:, b * T + q * BLK:b * T + (q + 1) * BLK])
                link(last)
                last = nc.vector.bn_aggr(gn_mv[:, b, :], gn_stats[:, b, :, :].rearrange("p q s -> p (q s)"))
            link(last)
            mean, var = gn_mv[:, :, 0], gn_mv[:, :, 1]
            nc.vector.tensor_copy(gn_ms[:, 0, :], mean)
            link(nc.vector.tensor_tensor(gn_w[:, 2, :], mean, mean, ALU.mult))
            nc.vector.tensor_tensor(gn_ms[:, 1, :], var, gn_w[:, 2, :], ALU.add).then_inc(gn_sums, 1)
            dve.wait_ge(gn_mean, 1)
            link(nc.vector.tensor_copy(gn_ms[:, :, :].rearrange("p k b -> p (k b)"), small_bank[:, 0:2 * B]))
            link(nc.vector.tensor_tensor(gn_w[:, 2, :], gn_ms[:, 0, :], gn_ms[:, 0, :], ALU.mult))
            nc.vector.tensor_tensor(gn_w[:, 0, :], gn_ms[:, 1, :], gn_w[:, 2, :], ALU.subtract).then_inc(gn_sums, 1)
            dve.wait_ge(gn_std, 1)
            link(nc.vector.reciprocal(gn_w[:, 2, :], gn_w[:, 1, :]))
            link(nc.vector.scalar_tensor_tensor(out=gn_w[:, 3, :], in0=gn_ms[:, 0, :], scalar=-1.0,
                                                in1=gn_w[:, 2, :], op0=ALU.mult, op1=ALU.mult))
            dve.wait_ge(alpha_ready, 1)

            def prepare(b):
                s = b % 2
                with dve.Fori(0, NB // 2) as i:
                    for h in range(2):
                        n = b * NB + 2 * i + h
                        dve.wait_ge(proj_done, n)
                        nc.vector.tensor_scalar(g_buf[h], X[:, cols(b, 2 * i + h)], gn_w[:, 2, b:b + 1],
                                                gn_w[:, 3, b:b + 1], ALU.mult, ALU.add).then_inc(g_ready, 1)
                    for h in range(2):
                        n = b * NB + 2 * i + h
                        q = blk(2 * i + h)
                        dve.wait_ge(relu_done, n + 2)
                        dve.wait_ge(hi_copied, n)
                        dve.wait_ge(split_done, n)
                        for j in range(3):
                            last = nc.vector.scalar_tensor_tensor(out=act_buf[j], in0=neg[j], scalar=neg_a[:, j:j + 1],
                                                                  in1=pos[j], op0=ALU.mult, op1=ALU.add)
                        last.then_inc(act_done, 1)
                        dve.wait_ge(act_done, n + 1)
                        nc.vector.tensor_copy(key_a[s][0:CH, q], act_buf[1][0:CH, :])
                        nc.vector.tensor_copy(hi_tmp[CH:C, :], act_buf[1][CH:C, :]).then_inc(lo_made, 1)
                        dve.wait_ge(lo_made, n + 1)
                        nc.vector.tensor_tensor(key_a[s][CH:C, q], act_buf[1][CH:C, :], hi_tmp[CH:C, :], ALU.subtract)
                        dve.wait_ge(hi_copied, n + 1)
                        nc.vector.tensor_tensor(query_b[s][0:CH, q], act_buf[0][0:CH, :], query_a[s][0:CH, q],
                                                ALU.subtract)
                        nc.vector.tensor_tensor(value_lo[s][:, q], act_buf[2], value_hi[s][:, q],
                                                ALU.subtract).then_inc(split_done, 1)

            def reduce_max(b, ib, p):
                v = b * 128 + ib * 16 + p
                dve.wait_ge(mx_ready, v + 1)
                nc.vector.reduce_max(part_max[:, bass.ds(ib * 16 + p, 1)], mx_bank, AX.X).then_inc(mx_read, 1)

            def finish_max(b):
                dve.wait_ge(mx_read, (b + 1) * 128)
                nc.vector.tensor_reduce(tile_max[:, :], part_max[:, :].rearrange("p (t k) -> p t k", k=4),
                                        AX.X, ALU.max).then_inc(max_found, 1)
                dve.wait_ge(max_turned, b + 1)
                if b:
                    dve.wait_ge(m_moved, 32 * b)
                turned = small_bank[0:T // 128, 0:128]
                link(nc.vector.tensor_scalar(m_hi[:, :], turned, -1.0 / MROW, None, ALU.mult))
                nc.vector.scalar_tensor_tensor(out=m_lo[:, :], in0=turned, scalar=-1.0 / MROW, in1=m_hi[:, :],
                                               op0=ALU.mult, op1=ALU.subtract).then_inc(m_ready, 1)

            def attend(m):
                mx = m + 1 < B

                def invert(ib):
                    dve.wait_ge(sums_ready, m * NB + ib + 1)
                    nc.vector.reciprocal(inv_sum[:, :], small_bank[:, 0:4]).then_inc(inv_ready, 1)

                def copy_rows(ib):
                    dve.wait_ge(inv_turned, m * NB + ib + 1)
                    nc.vector.tensor_copy(inv_rows[:, :], small_bank[0:4, 0:128]).then_inc(rows_ready, 1)

                def normalise(ib):
                    nb = m * NB + ib
                    dve.wait_ge(inv_spread, nb + 1)
                    dve.wait_ge(o_copied, nb + 1)
                    if m or not isinstance(ib, int) or ib:
                        dve.wait_ge(x_updated, nb)
                    nc.vector.tensor_tensor(o_norm, o_copy, small_bank, ALU.mult).then_inc(o_normed, 1)

                def body(ib, first):
                    for p in range(NP):
                        n = m * 128 + ib * 16 + p
                        if mx:
                            reduce_max(m + 1, ib, p)
                        dve.wait_ge(full_ready, n + 2)
                        dve.wait_ge(pv_done, n)
                        nc.vector.tensor_tensor(p_lo[p % 4], p_full[p % 2], p_hi[p % 4], ALU.subtract) \
                            .then_inc(lo_ready, 1)
                        if not first:
                            if p == 5:
                                invert(ib - 1)
                            if p == 7:
                                copy_rows(ib - 1)
                            if p == 9:
                                normalise(ib - 1)

                body(0, True)
                with dve.Fori(1, NB) as ib:
                    body(ib, False)
                invert(NB - 1)
                copy_rows(NB - 1)
                normalise(NB - 1)

            def channel_norm(k):
                b = k % B
                dve.wait_ge(u_ready, k * NB + 1)
                with dve.Fori(0, NB // 2) as i:
                    for h in range(2):
                        n = k * NB + 2 * i + h
                        dve.wait_ge(mean_ready, n + 1)
                        nc.vector.tensor_tensor(centered[:, blk(2 * i + h)], X[:, cols(b, 2 * i + h)], bank(h),
                                                ALU.subtract).then_inc(xc_ready, 1)
                dve.wait_ge(std_ready, k + 1)
                nc.vector.reciprocal(ln_rstd[:, :], ln_std[:, :]).then_inc(rstd_ready, 1)
                dve.wait_ge(rstd_turned, k + 1)
                nc.vector.tensor_copy(rstd_rows, PS[0:4, 3 * BLK:5 * BLK]).then_inc(rrows_ready, 1)
                with dve.Fori(0, NB // 2) as i:
                    for h in range(2):
                        n = k * NB + 2 * i + h
                        dve.wait_ge(rstd_spread, n + 1)
                        if k < B:
                            dve.wait_ge(ulo_ready, n)
                        else:
                            dve.wait_ge(wx_ready, n - B * NB)
                        nc.vector.tensor_tensor(normed[h], centered[:, blk(2 * i + h)], bank(h), ALU.mult) \
                            .then_inc(u_ready, 1)
                    for h in range(2):
                        n = k * NB + 2 * i + h
                        if k < B:
                            dve.wait_ge(uhi_ready, n + 2)
                            nc.vector.tensor_tensor(u_lo[b % 2][:, blk(2 * i + h)], normed[h],
                                                    u_hi[b % 2][:, blk(2 * i + h)], ALU.subtract) \
                                .then_inc(ulo_ready, 1)
                        else:
                            j = n - B * NB
                            dve.wait_ge(wx_stored, j + 2)
                            nc.vector.bn_stats(bn_st[:, bass.ds(j, 1), :], wx[:, cols(b, 2 * i + h)]) \
                                .then_inc(wx_counted, 1)

            prepare(0)
            with dve.Fori(0, NB) as ib:
                for p in range(16):
                    reduce_max(0, ib, p)
            finish_max(0)
            for m in range(B):
                if m + 1 < B:
                    prepare(m + 1)
                attend(m)
                if m + 1 < B:
                    finish_max(m + 1)
            for m in range(B, 2 * B):
                dve.wait_ge(x_updated, m * NB)
                channel_norm(m - B)
                attend(m)
            dve.wait_ge(x_updated, 2 * B * NB)
            for k in range(B, 2 * B):
                channel_norm(k)

            dve.wait_ge(wx_counted, B * NB + 1)
            nc.vector.bn_aggr(bn_mv[:, 0:2], bn_st[:, :, :].rearrange("p j s -> p (j s)")).then_inc(bn_var, 1)
            dve.wait_ge(bn_std, 1)
            link(nc.vector.reciprocal(bn_mv[:, 3:4], bn_mv[:, 2:3]))
            link(nc.vector.tensor_tensor(bn_mv[:, 4:5], bn_mv[:, 3:4], gb[:, 0:1], ALU.mult))
            link(nc.vector.tensor_tensor(bn_mv[:, 6:7], bn_mv[:, 0:1], bn_mv[:, 4:5], ALU.mult))
            nc.vector.tensor_tensor(bn_mv[:, 5:6], gb[:, 1:2], bn_mv[:, 6:7], ALU.subtract).then_inc(bn_ready, 1)
            dve.wait_ge(bn_ready, 1)
            gain = bn_mv[:, 4:5]

            def batch_cols(g, s):
                if s >= WARM:
                    return wx_steps[:, g * GC:(g + 1) * GC, s - WARM], 0
                return wx_steps[:, g * GC:(g + 1) * GC - 1, LEN - WARM + s], 1

            for s in range(WARM + LEN):
                for g in range(NG):
                    src, skip = batch_cols(g, s)
                    z = z_buf[:, g * GC + skip:(g + 1) * GC]
                    if s == 0:
                        if g == 0:
                            link(nc.vector.memset(z_buf[:, :], 0.0))
                        nc.vector.tensor_scalar(z, src, gain, None, ALU.mult).then_inc(z_ready[g], 1)
                    else:
                        dve.wait_ge(vy_ready[g], s)
                        nc.vector.scalar_tensor_tensor(out=z, in0=src, scalar=gain,
                                                       in1=bank(g)[:, skip:GC], op0=ALU.mult,
                                                       op1=ALU.add).then_inc(z_ready[g], 1)
                if s == WARM - 1:
                    for g in range(NG):
                        dve.wait_ge(y_ready[g], WARM)
                    nc.vector.memset(y_began[:, :].rearrange("p (b k) -> p b k", b=B)[:, :, 0:1], 0.0) \
                        .then_inc(start_set, 1)
            for g in range(NG):
                dve.wait_ge(y_ready[g], WARM + LEN)
            dve.wait_ge(start_set, 1)
            began = y_began[:, :].rearrange("p (b k) -> p b k", b=B)[:, :, 1:CHUNKS]
            ended = ys[:, LEN - 1, :].rearrange("p (b k) -> p b k", b=B)[:, :, 0:CHUNKS - 1]
            diff = z_buf[:, 0:B * (CHUNKS - 1)].rearrange("p (b k) -> p b k", b=B)
            link(nc.vector.tensor_tensor(diff, began, ended, ALU.subtract))
            link(nc.vector.tensor_tensor(diff, diff, diff, ALU.mult))
            link(nc.vector.tensor_scalar(diff, diff, CLOSE * CLOSE, None, ALU.is_le))
            nc.vector.tensor_reduce(gap[:, 0:1], diff, AX.XY, ALU.min).then_inc(gap_ready, 1)
            dve.wait_ge(gap_max, 1)
            link(nc.vector.tensor_reduce(gap[0:1, 1:2], small_bank[0:1, 0:128], AX.X, ALU.min))
            nc.vector.tensor_scalar(flag[0:1, 0:1], gap[0:1, 1:2], -1.0, 1.0, ALU.mult, ALU.add) \
                .then_inc(flag_ready, 1)
            dve.wait_ge(flag_ready, 1)
            far = dve.value_load(flag[0:1, 0:1], min_val=0, max_val=1)
            DONE = WARM + LEN
            with dve.If(far > 0):
                with dve.Fori(0, SEQ) as k:
                    for s in range(LEN):
                        dve.wait_ge(vy_ready[0], DONE - 1 + k * LEN + s + 1)
                        src = wx_steps[:, :, s].rearrange("p (b k) -> p b k", b=B)[:, :, bass.ds(k + 1, 1)]
                        nc.vector.scalar_tensor_tensor(
                            out=z_buf[:, 0:B].rearrange("p (b o) -> p b o", o=1), in0=src, scalar=gain,
                            in1=bank(0)[:, 0:B].rearrange("p (b o) -> p b o", o=1),
                            op0=ALU.mult, op1=ALU.add).then_inc(z_ready[0], 1)
                dve.wait_ge(y_ready[0], DONE + SEQ * LEN)
            for b in range(B):
                x_b = X[:, b * T:(b + 1) * T].rearrange("p (k s) -> p k s", s=LEN)
                y_b = ys[:, :, b * CHUNKS:(b + 1) * CHUNKS].rearrange("p s k -> p k s")
                nc.vector.tensor_tensor(x_b, x_b, y_b, ALU.add).then_inc(out_ready, 1)

        @block.gpsimd
        def _(pool):
            pool.sem_inc(sum_added, 1)
            made = [0]

            def link(ins):
                ins.then_inc(pool_step, 1)
                made[0] += 1
                pool.wait_ge(pool_step, made[0])

            nc.gpsimd.memset(ones[:, :], 1.0)
            nc.gpsimd.memset(eps_gn[:, :], 1e-5)
            nc.gpsimd.memset(lift[:, 0:1], LIFT)
            nc.gpsimd.memset(lift[:, 1:2], LIFT - ROWMAX)
            nc.gpsimd.memset(channel_mean[:, :], 1.0 / C)
            nc.gpsimd.memset(ident[:, :], 0.0)
            link(nc.gpsimd.memset(group_mean[:, :], 1.0 / GROUP))
            for s in range(2):
                link(nc.gpsimd.memset(key_b[s][CH:CH + 2, :], MROW))
            link(nc.gpsimd.memset(select[:, :, :], 0.0))
            nc.gpsimd.affine_select(out=ident[:, :], in_=ident[:, :], compare_op=ALU.not_equal, fill=1.0,
                                    base=0, pattern=[[-1, C]], channel_multiplier=1)
            nc.gpsimd.affine_select(out=select[:, :, :], in_=select[:, :, :], compare_op=ALU.not_equal, fill=1.0,
                                    base=0, pattern=[[-1, 4], [0, C]], channel_multiplier=1)
            gm = group_mean[:, :].rearrange("p (g r) -> p g r", r=GROUP)
            link(nc.gpsimd.affine_select(out=gm, in_=gm, compare_op=ALU.is_ge, fill=0.0, base=0,
                                         pattern=[[-GROUP, C // GROUP], [0, GROUP]], channel_multiplier=1))
            link(nc.gpsimd.affine_select(out=gm, in_=gm, compare_op=ALU.is_ge, fill=0.0, base=GROUP - 1,
                                         pattern=[[GROUP, C // GROUP], [0, GROUP]], channel_multiplier=-1))
            nc.gpsimd.tensor_copy(ident16[:, :], ident[:, :]).then_inc(consts_set, 1)

            def prepare(b):
                s = b % 2
                with pool.Fori(0, NB // 2) as i:
                    for h in range(2):
                        n = b * NB + 2 * i + h
                        q = blk(2 * i + h)
                        pool.wait_ge(act_done, n + 1)
                        nc.gpsimd.tensor_copy(query_a[s][:, q], act_buf[0])
                        nc.gpsimd.tensor_copy(value_hi[s][:, q], act_buf[2])
                        nc.gpsimd.tensor_copy(key_b[s][0:CH, q], act_buf[1][0:CH, :]).then_inc(hi_copied, 1)

            def attend(m):
                b = m % B

                def update(ib):
                    nb = m * NB + ib
                    pool.wait_ge(o_normed, nb + 2)
                    nc.gpsimd.tensor_tensor(X[:, cols(b, ib)], X[:, cols(b, ib)], o_norm, ALU.add) \
                        .then_inc(x_updated, 1)

                def body(ib, first):
                    for p in range(NP):
                        nb = m * NB + ib
                        n = nb * 16 + p
                        halves = p_full[p % 2][:, 0:BLK], p_full[p % 2][:, BLK:2 * BLK]
                        pool.wait_ge(full_ready, n + 2)
                        pool.wait_ge(sum_added, n + 1)
                        if p == 0:
                            nc.gpsimd.tensor_tensor(sum_run, halves[0], halves[1], ALU.add).then_inc(sum_added, 1)
                        else:
                            nc.gpsimd.tensor_tensor(sum_run, sum_run, halves[0], ALU.add).then_inc(sum_half, 1)
                            pool.wait_ge(sum_half, nb * 15 + p)
                            if p == NP - 1 and (m or not first):
                                pool.wait_ge(sums_ready, nb)
                            nc.gpsimd.tensor_tensor(sum_run if p < NP - 1 else sum_end, sum_run, halves[1],
                                                    ALU.add).then_inc(sum_added, 1)
                        if p == 10 and not first:
                            update(ib - 1)

                body(0, True)
                with pool.Fori(1, NB) as ib:
                    body(ib, False)
                update(NB - 1)

            prepare(0)
            for m in range(B):
                if m + 1 < B:
                    prepare(m + 1)
                attend(m)
            for m in range(B, 2 * B):
                attend(m)


_INS = ['x', 'L0_conv_w1', 'L0_conv_b1', 'L0_conv_a1', 'L0_conv_w2', 'L0_conv_b2', 'L0_conv_a2', 'L0_conv_wa',
        'L0_conv_ba', 'L0_conv_aa', 'L1_ffn_W', 'L1_ffn_V', 'L1_ffn_gamma', 'L1_ffn_beta']


def kernel(**inputs):
    import numpy as _np
    import concourse.bacc as _bacc
    from concourse import mybir as _mybir
    from concourse.bass_utils import run_bass_kernel_spmd as _run

    nc = _bacc.Bacc("TRN2", target_bir_lowering=False, num_devices=1)
    n, c, h, w = inputs["x"].shape
    shapes = {"x": (n, c, h * w), "L0_conv_ba": (1, c)}
    arrays, args = {}, []
    for name in _INS:
        a = _np.ascontiguousarray(inputs[name])
        if name in shapes:
            a = a.reshape(shapes[name])
        elif a.ndim < 2:
            a = a.reshape(-1, 1)
        arrays[f"in_{name}"] = a
        args.append(nc.dram_tensor(f"in_{name}", a.shape, _mybir.dt.from_np(a.dtype), kind="ExternalInput").ap())
    args.append(nc.dram_tensor("out_0", (n, c, h * w), _mybir.dt.float32, kind="ExternalOutput").ap())
    hybrid_kernel(nc, *args)
    r = _run(nc, [arrays], core_ids=[0])
    return r.results[0]["out_0"].reshape(n, c, h, w)
```

```python
import concourse.bass as bass
from concourse import mybir
from contextlib import ExitStack
from math import log

F32 = mybir.dt.float32
F16 = mybir.dt.float16
I32 = mybir.dt.int32
ACT = mybir.ActivationFunctionType
ALU = mybir.AluOpType
AX = mybir.AxisListType


def hybrid_kernel(nc, x, w1, b1, a1, w2, b2, a2, wa, ba, aa, W, V, gamma, beta, out):
    B, C, T = x.shape
    CH = w1.shape[0]
    BLK = 512
    NB = T // BLK
    NP = T // 256
    GROUP = C // 32
    HALF = BLK // 2
    LIFT = 6.0 * log(2.0)
    MROW = 64.0
    ROWMAX = float(C) ** 0.5
    LEN = 32
    CHUNKS = T // LEN
    WARM = 12
    COLS = B * CHUNKS
    NG = 2
    GC = COLS // NG
    GB = B // NG
    CLOSE = 2.0 ** -18
    assert C == 128 and CH == 64 and T == 4096 and B == 4 and COLS == 512

    with ExitStack() as ctx:
        def sb(name, shape, dt=F32):
            return ctx.enter_context(nc.sbuf_tensor(name, shape, dt))

        def signal(name):
            return ctx.enter_context(nc.semaphore(name))

        X = sb("X", [C, B * T])
        REG = sb("REG", [C, 32768])

        def f32(at, n):
            return REG[:, at:at + n]

        def f16(at, n):
            return REG[:, at:at + n // 2].bitcast(F16)

        SET = 12288
        key_a = [f16(s * SET, T) for s in range(2)]
        key_b = [f16(s * SET + 2048, T) for s in range(2)]
        query_a = [f16(s * SET + 4096, T) for s in range(2)]
        query_b = [f16(s * SET + 6144, T) for s in range(2)]
        value_hi = [f16(s * SET + 8192, T) for s in range(2)]
        value_lo = [f16(s * SET + 10240, T) for s in range(2)]
        u_hi = [f16(0, T), f16(16384, T)]
        u_lo = [f16(2048, T), f16(18432, T)]
        t_hi = [f16(8192, T), f16(20480, T)]
        t_lo = [f16(10240, T), f16(22528, T)]
        WORK = 2 * SET
        p_hi = [f16(WORK + 512 * j, 1024) for j in range(4)]
        p_lo = [f16(WORK + 2048 + 512 * j, 1024) for j in range(2)]
        p_full = [f32(WORK + 3072 + 1024 * j, 1024) for j in range(2)]
        sum_run, sum_end = f32(WORK + 5120, 1024), f32(WORK + 6144, 1024)
        o_copy, o_norm = f32(WORK + 7168, BLK), f32(WORK + 7680, BLK)
        pos = [[f32(WORK + 1536 * h + 512 * j, BLK) for j in range(3)] for h in range(2)]
        neg = [f32(WORK + 3072 + 512 * j, BLK) for j in range(3)]
        hi_tmp = f16(WORK + 4608, BLK)
        WX_SLOT = [1, 3, 0, 2]
        wx = f32(0, B * T)
        ys = f32(B * T, B * T).rearrange("p (s c) -> p s c", c=COLS)

        w_t = sb("w_t", [C, 5, C])
        w_in = f32(WORK + 5120, 5 * C).rearrange("p (j c) -> p j c", c=C)
        w1_t, w2_t, wa_t, W_t, V_t = [w_t[:, j, :] for j in range(5)]
        ident = sb("ident", [C, C])
        ident16 = sb("ident16", [C, C], F16)
        group_mean = sb("group_mean", [C, C])
        scratch = sb("scratch", [C, 4, BLK])
        ones = sb("ones", [C, C])
        zero = sb("zero", [C, 1])
        ba_row = sb("ba_row", [1, C])
        a_row = sb("a_row", [1, 4])
        bias12 = sb("bias12", [C, 2])
        neg_a = sb("neg_a", [C, 4])
        lift = sb("lift", [C, 2])
        gb = sb("gb", [C, 2])
        gn_st = sb("gn_st", [C, NB, 6])
        gn_mv = sb("gn_mv", [C, 2])
        gn_ms = sb("gn_ms", [C, 2])
        gn_w = sb("gn_w", [C, 5])
        w_s = scratch[:, 1, 0:3 * C].rearrange("p (j c) -> p j c", c=C)
        bias_s = sb("bias_s", [C, 4])
        ba_s = scratch[0:1, 1, 3 * C:4 * C]
        inv_sum = sb("inv_sum", [C, 4])
        lane_st = sb("lane_st", [C, 16, 6])
        lane_mv = sb("lane_mv", [C, 16, 2])
        lane_w = sb("lane_w", [C, 3, 16])
        bn_st = sb("bn_st", [C, B * NB, 6])
        bn_mv = sb("bn_mv", [C, 10])
        inv_rows = sb("inv_rows", [4, C])
        part_max = scratch[:, 3, 0:16]
        tile_max = scratch[:, 3, 16:20]
        m_hi = scratch[0:4, 3, 64:128].bitcast(F16)
        m_lo = scratch[0:4, 3, 128:192].bitcast(F16)
        lane_bank = (7, 6, 0, 1)
        lane_x = [scratch[:, 0, :], scratch[:, 1, :], f32(WORK, BLK), f32(WORK + 512, BLK)]
        lane_t = [scratch[:, 2, :], scratch[:, 3, :], f32(WORK + 1024, BLK), f32(WORK + 1536, BLK)]
        y_began = scratch[:, 0, :]
        z_buf = scratch[:, 1, :]
        gap = sb("gap", [C, 4])
        flag = sb("flag", [1, 1], I32)

        PS = ctx.enter_context(nc.psum_tensor("PS", [C, 8 * BLK], F32))

        def bank(j, n=1):
            return PS[:, j * BLK:(j + n) * BLK]

        o_bank, mx_bank, small_bank = bank(4), bank(5, 2), bank(7)
        proj_bank = [bank(j) for j in (0, 1, 2, 3, 5, 6)]

        x_loaded = [signal(f"x_loaded{b}") for b in range(B)]
        w_loaded = signal("w_loaded")
        consts_set = signal("consts_set")
        w_turned = signal("w_turned")
        w_ready = signal("w_ready")
        alpha_ready = signal("alpha_ready")
        dve_step = signal("dve_step")
        pool_step = signal("pool_step")
        gn_sums = signal("gn_sums")
        gn_mean = signal("gn_mean")
        gn_counted = signal("gn_counted")
        gn_scaled = signal("gn_scaled")
        gn_shift = signal("gn_shift")
        gn_done = signal("gn_done")
        proj_done = signal("proj_done")
        relu_done = signal("relu_done")
        act_done = signal("act_done")
        query_copied = signal("query_copied")
        key_copied = signal("key_copied")
        key_split = signal("key_split")
        query_split = signal("query_split")
        value_copied = signal("value_copied")
        value_split = signal("value_split")
        mx_ready = signal("mx_ready")
        mx_read = signal("mx_read")
        max_found = signal("max_found")
        max_turned = signal("max_turned")
        m_hi_made = signal("m_hi_made")
        m_ready = signal("m_ready")
        m_moved = signal("m_moved")
        scores_ready = signal("scores_ready")
        hi_ready = signal("hi_ready")
        full_ready = signal("full_ready")
        lo_ready = signal("lo_ready")
        pv_done = signal("pv_done")
        sum_added = signal("sum_added")
        o_copied = signal("o_copied")
        sums_ready = signal("sums_ready")
        inv_ready = signal("inv_ready")
        inv_turned = signal("inv_turned")
        rows_ready = signal("rows_ready")
        inv_spread = signal("inv_spread")
        o_normed = signal("o_normed")
        x_updated = signal("x_updated")
        lanes = range(4)
        lane_staged = [signal(f"lane_staged{l}") for l in range(2)]
        lane_turned = [signal(f"lane_turned{l}") for l in lanes]
        lane_step = [signal(f"lane_step{l}") for l in lanes]
        lane_normed = [signal(f"lane_normed{l}") for l in lanes]
        lane_back = [signal(f"lane_back{l}") for l in lanes]
        lane_copied = [signal(f"lane_copied{l}") for l in lanes]
        lane_done = [signal(f"lane_done{l}") for l in lanes]
        lane_stored = [signal(f"lane_stored{l}") for l in lanes]
        t_hi_ready = signal("t_hi_ready")
        t_lo_ready = signal("t_lo_ready")
        wx_counted = signal("wx_counted")
        bn_ready = signal("bn_ready")
        vy_ready = [signal(f"vy_ready{g}") for g in range(NG)]
        z_ready = [signal(f"z_ready{g}") for g in range(NG)]
        y_ready = [signal(f"y_ready{g}") for g in range(NG)]
        start_set = signal("start_set")
        gap_ready = signal("gap_ready")
        gap_max = signal("gap_max")
        flag_ready = signal("flag_ready")
        out_ready = signal("out_ready")
        stored = signal("stored")

        block = ctx.enter_context(nc.Block())
        x_v = x.rearrange("b c t -> c b t")
        out_v = out.rearrange("b c t -> c b t")

        def cols(b, q):
            return bass.ds(b * T + q * BLK, BLK)

        def blk(q):
            return bass.ds(q * BLK, BLK)

        wx_steps = wx.rearrange("p (n s) -> p n s", s=LEN)
        GUESS = float(0x5f3759df)
        RSQRT = 12
        STEPS = RSQRT + 2

        def jobs(m):
            found = []
            if B - 1 <= m < 2 * B - 1:
                found.append((0, "tokens", m - (B - 1), (m - (B - 1)) * NB))
            if m > B:
                found.append((1, "ffn", m - B - 1, (m - B - 1) * NB))
            return found

        LAST = [[(l, B - 1, (B * NB, (B - 1) * NB, 0, 0)[l] + r, 4 * r + l) for l in lanes] for r in range(NB // 4)]

        LEAD = 24
        PAUSE = NB - 2

        def max_unit(m, ib, p):
            block, unit = (ib + 1, p + 8) if p < 8 else (ib + 2, p - 8)
            if isinstance(block, int) and block >= NB:
                m, block = m + 1, block - NB
            return (m, block, unit) if m < B else None

        def ffn_job(l, j):
            return j - B * NB if l == 0 else j

        def wx_cols(b, q):
            return bass.ds(WX_SLOT[b] * T + q * BLK, BLK)

        def before(m, ib):
            return (m, ib - 1) if not isinstance(ib, int) or ib else (m - 1, NB - 1)

        SEQ = CHUNKS - 1

        def state(s):
            if s >= WARM:
                return ys[:, s - WARM, :]
            return y_began if s == WARM - 1 else ys[:, LEN // 2 + s % 2, :]

        def seq_cols(buf, s, k):
            return buf[:, s, :].rearrange("p (b k) -> p b k", b=B)[:, :, bass.ds(k, 1)]

        @block.sync
        def _(sp):
            for b in range(B):
                sp.dma_start(X[:, b * T:(b + 1) * T], x[b]).then_inc(x_loaded[b], 16)
                if b == 0:
                    for half in range(2):
                        rows = slice(CH * half, CH * half + CH)
                        sp.dma_start(w_in[rows, 0, :], w1).then_inc(w_loaded, 16)
                        sp.dma_start(w_in[rows, 1, :], w2).then_inc(w_loaded, 16)
                        sp.dma_start(bias12[rows, 0:1], b1).then_inc(w_loaded, 16)
                        sp.dma_start(bias12[rows, 1:2], b2).then_inc(w_loaded, 16)
                    for j, w in enumerate((wa, W, V)):
                        sp.dma_start(w_in[:, 2 + j, :], w).then_inc(w_loaded, 16)
                    sp.dma_start(gb[:, 0:1], gamma).then_inc(w_loaded, 16)
                    sp.dma_start(gb[:, 1:2], beta).then_inc(w_loaded, 16)
                    sp.dma_start(ba_row[:, :], ba).then_inc(w_loaded, 16)
                    for j, a in enumerate((a1, a2, aa)):
                        sp.dma_start(a_row[0:1, j:j + 1], a).then_inc(w_loaded, 16)
            for b in range(B):
                with sp.Fori(0, NB) as ib:
                    for row, part in ((CH, m_hi), (CH + 1, m_lo)):
                        if row == CH:
                            sp.wait_ge(m_ready, b * NB + ib + 1)
                        sp.dma_start(query_b[b % 2][row:row + 1, blk(ib)].rearrange("o (t p) -> o t p", p=128),
                                     part).then_inc(m_moved, 16)
            for b in range(B):
                sp.wait_ge(out_ready, b + 1)
                sp.dma_start(out[b], X[:, b * T:(b + 1) * T]).then_inc(stored, 16)
            sp.wait_ge(stored, 16 * B)

        W_LOADS = 16 * (8 + 3 + 3 + 3)

        @block.tensor
        def _(pe):
            pe.sem_inc(proj_done, 1)
            pe.sem_inc(pv_done, 3)

            pe.wait_ge(w_loaded, W_LOADS)
            pe.wait_ge(consts_set, 1)
            for j in range(5):
                last = nc.tensor.transpose(PS[:, j * C:(j + 1) * C], w_in[:, j, :], ident[:, :])
            last.then_inc(w_turned, 1)
            nc.tensor.matmul(small_bank[:, 0:3], ones[0:1, :], a_row[0:1, 0:3], start=True, stop=True) \
                .then_inc(w_turned, 1)
            pe.wait_ge(w_ready, 1)
            pe.wait_ge(alpha_ready, 1)

            def gn_group(b):
                if b:
                    pe.wait_ge(o_normed, (b - 1) * NB + 1)
                    pe.wait_ge(m_ready, (b - 1) * NB + 2)
                pe.wait_ge(gn_sums, b + 1)
                nc.tensor.matmul(small_bank[:, 0:2], group_mean[:, :], gn_ms[:, :], start=True, stop=True) \
                    .then_inc(gn_mean, 1)

            def gn_biases(b):
                if b:
                    pe.wait_ge(o_normed, (b - 1) * NB + PAUSE)
                    pe.wait_ge(m_ready, (b - 1) * NB + PAUSE + 1)
                pe.wait_ge(gn_scaled, b + 1)
                shift = gn_w[:, 3:4]
                nc.tensor.matmul(small_bank[:, 0:1], w1_t, shift, start=True, stop=True)
                nc.tensor.matmul(small_bank[:, 1:2], w2_t, shift, start=True, stop=True)
                nc.tensor.matmul(small_bank[0:1, 128:256], shift, wa_t, start=True, stop=True).then_inc(gn_shift, 1)

            def prepare(b):
                gn_biases(b)
                pe.wait_ge(gn_done, b + 1)
                if b:
                    done = ((b - 1) * NB + PAUSE) * 16
                    pe.wait_ge(full_ready, done + 1)
                    pe.wait_ge(mx_read, done + LEAD)
                for q in range(NB):
                    h, x_q = q % 2, X[:, b * T + q * BLK:b * T + (q + 1) * BLK]
                    pe.wait_ge(relu_done, b * NB + q)
                    nc.tensor.matmul(proj_bank[3 * h], w_s[:, 0, :], x_q, start=True, stop=True)
                    nc.tensor.matmul(proj_bank[3 * h + 1], w_s[:, 1, :], x_q, start=True, stop=True)
                    for t in range(4):
                        o = proj_bank[3 * h + 2][:, t * C:(t + 1) * C]
                        nc.tensor.matmul(o, x_q[:, t * 128:(t + 1) * 128], w_s[:, 2, :], start=True, stop=False)
                        last = nc.tensor.matmul(o, ones[0:1, :], ba_s, start=False, stop=True)
                    last.then_inc(proj_done, 1)
                pe.wait_ge(query_split, (b + 1) * NB + 2)
                pe.wait_ge(value_split, (b + 1) * NB + 2)

            def max_scores(b, ib, p):
                v = b * 128 + ib * 16 + p
                pe.wait_ge(mx_read, v)
                for t in range(2):
                    last = nc.tensor.matmul(mx_bank[:, t * BLK:(t + 1) * BLK],
                                            query_a[b % 2][:, bass.ds(ib * BLK + p // 4 * 128, 128)],
                                            key_a[b % 2][:, (p % 4 * 2 + t) * BLK:(p % 4 * 2 + t + 1) * BLK],
                                            start=True, stop=True)
                last.then_inc(mx_ready, 1)

            def turn_max(g):
                pe.wait_ge(max_found, g + 1)
                nc.tensor.transpose(small_bank[0:4, 0:128], tile_max, ident[:, :]).then_inc(max_turned, 1)

            def products(m):
                s = m % 2
                if m < B:
                    return [(key_a[s], query_a[s], C), (key_b[s], query_b[s], CH + 2)], value_hi[s], value_lo[s]
                return [(u_hi[s], u_hi[s], C), (u_hi[s], u_lo[s], C), (u_lo[s], u_hi[s], C)], t_hi[s], t_lo[s]

            def scores(m, ib, p):
                n = m * 128 + ib * 16 + p
                score_terms = products(m)[0]
                if m < B and p == 0:
                    pe.wait_ge(m_moved, 32 * (m * NB + ib + 1))
                pe.wait_ge(full_ready, n)
                for t in range(2):
                    j = 2 * p + t
                    for k, (key, query, rows) in enumerate(score_terms):
                        last = nc.tensor.matmul(bank(p % 2 * 2 + t), key[0:rows, j * 128:(j + 1) * 128],
                                                query[0:rows, blk(ib)], start=(k == 0),
                                                stop=(k == len(score_terms) - 1))
                last.then_inc(scores_ready, 1)

            def weigh(m, ib, p):
                n = m * 128 + ib * 16 + p
                v_hi, v_lo = products(m)[1:]
                pe.wait_ge(hi_ready, n + 1)
                if p == 0:
                    pe.wait_ge(o_copied, m * NB + ib)
                for v in (v_hi, v_lo):
                    for t in range(2):
                        j = 2 * p + t
                        nc.tensor.matmul(o_bank, v[:, j * 128:(j + 1) * 128], p_hi[p % 4][:, t * BLK:(t + 1) * BLK],
                                         start=(p == 0 and t == 0 and v is v_hi), stop=False)
                pe.wait_ge(lo_ready, n + 2)
                for t in range(2):
                    j = 2 * p + t
                    last = nc.tensor.matmul(o_bank, v_hi[:, j * 128:(j + 1) * 128],
                                            p_lo[p % 2][:, t * BLK:(t + 1) * BLK],
                                            start=False, stop=(p == NP - 1 and t == 1))
                last.then_inc(pv_done, 1)

            def column_sums(m, ib, others=()):
                nb = m * NB + ib
                pe.wait_ge(sum_added, (nb + 1) * 16 + 1)
                pe.wait_ge(o_normed, nb + 1)
                for sem, events in others:
                    pe.wait_ge(sem, events)
                for t in range(4):
                    for h in range(2):
                        last = nc.tensor.matmul(small_bank[:, t:t + 1],
                                                sum_end[:, h * BLK + t * 128:h * BLK + (t + 1) * 128],
                                                ones[:, 0:1], start=(h == 0), stop=(h == 1))
                last.then_inc(sums_ready, 1)

            def turn_inverse(m, ib):
                pe.wait_ge(inv_ready, m * NB + ib + 1)
                nc.tensor.transpose(small_bank[0:4, 0:128], inv_sum[:, :], ident[:, :]).then_inc(inv_turned, 1)

            def spread(dst, rows):
                for t in range(4):
                    last = nc.tensor.matmul(dst[:, t * 128:(t + 1) * 128], ident[0:4, t:t + 1].broadcast_to([4, C]),
                                            rows, start=True, stop=True)
                return last

            def spread_inverse(m, ib):
                pe.wait_ge(rows_ready, m * NB + ib + 1)
                spread(small_bank, inv_rows[:, :]).then_inc(inv_spread, 1)

            def lane_turn(l, x_q, j, staged):
                if staged:
                    pe.wait_ge(lane_staged[l], j + 1)
                pe.wait_ge(lane_stored[l], j)
                for t in range(4):
                    last = nc.tensor.transpose(bank(lane_bank[l])[:, t * 128:(t + 1) * 128],
                                               x_q[:, t * 128:(t + 1) * 128], ident[:, :])
                last.then_inc(lane_turned[l], 1)

            def lane_return(l, j):
                pe.wait_ge(lane_normed[l], j + 1)
                for t in range(4):
                    last = nc.tensor.transpose(bank(lane_bank[l])[:, t * 128:(t + 1) * 128],
                                               lane_t[l][:, t * 128:(t + 1) * 128], ident[:, :])
                last.then_inc(lane_back[l], 1)

            def lane_product(l, kind, b, q, j):
                if kind == "tokens":
                    pe.wait_ge(t_lo_ready, j + 1)
                    turned = bank(lane_bank[l]).bitcast(F16)
                    for part, src in enumerate((t_hi, t_lo)):
                        for t in range(4):
                            last = nc.tensor.transpose(turned[:, part * BLK + t * 128:part * BLK + (t + 1) * 128],
                                                       src[b % 2][:, bass.ds(q * BLK + t * 128, 128)],
                                                       ident16[:, :])
                else:
                    pe.wait_ge(lane_copied[l], ffn_job(l, j) + 1)
                    last = nc.tensor.matmul(bank(lane_bank[l]), W_t, lane_x[l], start=True, stop=True)
                last.then_inc(lane_done[l], 1)

            def attend(m, follows):
                def body(ib):
                    has_before = follows or not isinstance(ib, int) or ib > 0
                    resumes = m + 1 < B and isinstance(ib, int) and ib == PAUSE
                    pm, pb = before(m, ib)
                    nb = m * NB + ib
                    chained = m < B - 1 or m == B - 1 and not (isinstance(ib, int) and ib == NB - 1)
                    others = []
                    if m < B - 1 and not (isinstance(ib, int) and ib == 0):
                        others.append((gn_scaled, m + 2))
                    for l, kind, b, j0 in jobs(m):
                        if kind == "tokens":
                            others.append((lane_normed[l], j0 + ib + 1))
                    for p in range(NP):
                        scores(m, ib, p)
                        unit = max_unit(m, ib, p)
                        if unit:
                            max_scores(*unit)
                        if p >= 2:
                            weigh(m, ib, p - 2)
                        elif has_before and not resumes:
                            weigh(pm, pb, NP + p - 2)
                        if has_before:
                            if p == 5:
                                column_sums(pm, pb, others)
                            if p == 7:
                                turn_inverse(pm, pb)
                            if p == 9:
                                spread_inverse(pm, pb)
                        if p == 11 and chained:
                            pe.wait_ge(o_normed, nb + 1)
                            turn_max(nb + 1)
                        for l, kind, b, j0 in jobs(m):
                            j = j0 + ib
                            if p == 2 + l:
                                lane_turn(l, lane_x[l], j, True)
                            if p == 7 + l and kind == "ffn":
                                lane_return(l, j)
                            if p == 13:
                                if kind == "tokens":
                                    pe.wait_ge(o_normed, nb + 1)
                                    if chained:
                                        pe.wait_ge(m_ready, nb + 2)
                                lane_product(l, kind, b, ib, j)
                        if p == NP - 1 and m + 1 < B and isinstance(ib, int) and ib == 0:
                            gn_group(m + 1)

                body(0)
                if m < B:
                    with pe.Fori(1, PAUSE) as ib:
                        body(ib)
                    if m + 1 < B:
                        weigh(m, PAUSE - 1, NP - 2)
                        weigh(m, PAUSE - 1, NP - 1)
                        prepare(m + 1)
                    body(PAUSE)
                    body(PAUSE + 1)
                else:
                    with pe.Fori(1, NB) as ib:
                        body(ib)

            def finish(m):
                weigh(m, NB - 1, NP - 2)
                weigh(m, NB - 1, NP - 1)
                column_sums(m, NB - 1)
                turn_inverse(m, NB - 1)
                spread_inverse(m, NB - 1)

            gn_group(0)
            prepare(0)
            for v in range(LEAD):
                max_scores(0, v // 16, v % 16)
                if v == 17:
                    turn_max(0)
            for m in range(2 * B):
                if m >= B:
                    pe.wait_ge(lane_stored[0], (m - B + 1) * NB)
                attend(m, follows=m > 0)
            finish(2 * B - 1)
            pe.wait_ge(x_updated, 2 * B * NB)
            for batch_jobs in LAST:
                for l, b, j, q in batch_jobs:
                    lane_turn(l, X[:, b * T + q * BLK:b * T + (q + 1) * BLK], j, False)
                for l, b, j, q in batch_jobs:
                    lane_return(l, j)
                for l, b, j, q in batch_jobs:
                    lane_product(l, "ffn", b, q, j)

            pe.wait_ge(bn_ready, 1)
            for s in range(1, WARM + LEN):
                for g in range(NG):
                    gs = slice(g * GC, (g + 1) * GC)
                    prev = state(s - 1)[:, gs]
                    pe.wait_ge(y_ready[g], s)
                    if s == WARM:
                        pe.wait_ge(start_set, 1)
                    nc.tensor.matmul(bank(g)[:, 0:GC], V_t, prev, start=True, stop=True) \
                        .then_inc(vy_ready[g], 1)
            pe.wait_ge(gap_ready, 1)
            nc.tensor.transpose(small_bank[0:1, 0:128], gap[:, 0:1], ident[:, :]).then_inc(gap_max, 1)
            pe.wait_ge(flag_ready, 1)
            far = pe.value_load(flag[0:1, 0:1], min_val=0, max_val=1)
            DONE = WARM + LEN
            with pe.If(far > 0):
                with pe.Fori(0, SEQ) as k:
                    for s in range(LEN):
                        prev = seq_cols(ys, (s - 1) % LEN, k + (1 if s else 0))
                        pe.wait_ge(y_ready[0], DONE + k * LEN + s)
                        nc.tensor.matmul(bank(0)[:, 0:B], V_t, prev, start=True, stop=True) \
                            .then_inc(vy_ready[0], 1)

        @block.scalar
        def _(act):
            act.sem_inc(relu_done, 1)
            act.sem_inc(full_ready, 1)
            act.wait_ge(w_turned, 1)
            nc.scalar.activation(w_t[:, :, :].rearrange("p j c -> p (j c)"), PS[:, 0:5 * C], ACT.Copy) \
                .then_inc(w_ready, 1)
            act.wait_ge(w_turned, 2)
            nc.scalar.activation(neg_a[:, 0:3], small_bank[:, 0:3], ACT.Copy, scale=-1.0) \
                .then_inc(alpha_ready, 1)

            def prepare(b):
                s = b % 2
                act.wait_ge(gn_done, b + 1)
                if b:
                    done = ((b - 1) * NB + PAUSE) * 16
                    act.wait_ge(pv_done, done + 3)
                    act.wait_ge(lo_ready, done + 1)
                    act.wait_ge(sum_added, done + 1)
                else:
                    act.wait_ge(alpha_ready, 1)
                with act.Fori(0, NB // 2) as i:
                    for h in range(2):
                        n = b * NB + 2 * i + h
                        src = proj_bank[3 * h:3 * h + 3]
                        act.wait_ge(proj_done, n + 2)
                        act.wait_ge(query_split, n + 1)
                        act.wait_ge(value_split, n + 1)
                        for j in range(3):
                            nc.scalar.activation(pos[h][j], src[j], ACT.Relu, bias=bias_s[:, j:j + 1] if j < 2 else 0.0)
                        act.wait_ge(act_done, n + 1)
                        for j in range(3):
                            last = nc.scalar.activation(neg[j], src[j], ACT.Relu, scale=-1.0,
                                                        bias=bias_s[:, 2 + j:3 + j] if j < 2 else 0.0)
                        last.then_inc(relu_done, 1)
                    for h in range(2):
                        n = b * NB + 2 * i + h
                        act.wait_ge(act_done, n + 2)
                        nc.scalar.activation(query_a[s][:, blk(2 * i + h)], pos[h][0], ACT.Copy) \
                            .then_inc(query_copied, 1)

            def lane_hi(l, b, q, j):
                act.wait_ge(lane_normed[l], j + 1)
                nc.scalar.activation(t_hi[b % 2][:, blk(q)], lane_t[l], ACT.Copy).then_inc(t_hi_ready, 1)

            def lane_copy(l, j):
                act.wait_ge(lane_back[l], ffn_job(l, j) + 1)
                nc.scalar.activation(lane_x[l], bank(lane_bank[l]), ACT.Copy).then_inc(lane_copied[l], 1)

            def lane_store(l, kind, b, q, j):
                act.wait_ge(lane_done[l], j + 1)
                if kind == "tokens":
                    turned = bank(lane_bank[l]).bitcast(F16)
                    nc.scalar.activation(u_hi[b % 2][:, blk(q)], turned[:, 0:BLK], ACT.Copy)
                    last = nc.scalar.activation(u_lo[b % 2][:, blk(q)], turned[:, BLK:2 * BLK], ACT.Copy)
                else:
                    last = nc.scalar.activation(wx[:, wx_cols(b, q)], bank(lane_bank[l]), ACT.Copy)
                last.then_inc(lane_stored[l], 1)

            def copy_out(m, ib):
                nb = m * NB + ib
                act.wait_ge(pv_done, (nb + 1) * 16 + 3)
                act.wait_ge(o_normed, nb + 1)
                nc.scalar.activation(o_copy, o_bank, ACT.Copy).then_inc(o_copied, 1)

            def attend(m, follows):
                scale = 1.0 if m < B else C ** -0.5
                bias = lift[:, 0:1] if m < B else lift[:, 1:2]

                def body(ib):
                    has_before = follows or not isinstance(ib, int) or ib > 0
                    for p in range(NP):
                        n = m * 128 + ib * 16 + p
                        src = bank(p % 2 * 2, 2)
                        act.wait_ge(scores_ready, n + 1)
                        act.wait_ge(pv_done, n)
                        nc.scalar.activation(p_hi[p % 4], src, ACT.Exp, bias=bias, scale=scale) \
                            .then_inc(hi_ready, 1)
                        act.wait_ge(lo_ready, n)
                        act.wait_ge(sum_added, n)
                        nc.scalar.activation(p_full[p % 2], src, ACT.Exp, bias=bias, scale=scale) \
                            .then_inc(full_ready, 1)
                        if p == 1 and has_before:
                            copy_out(*before(m, ib))
                        for l, kind, b, j0 in jobs(m):
                            j = j0 + ib
                            if p == 5 and kind == "tokens":
                                lane_hi(l, b, ib, j)
                            if p == 8 + l and kind == "ffn":
                                lane_copy(l, j)
                            if p == 14:
                                lane_store(l, kind, b, ib, j)

                body(0)
                if m < B:
                    with act.Fori(1, PAUSE) as ib:
                        body(ib)
                    if m + 1 < B:
                        prepare(m + 1)
                    body(PAUSE)
                    body(PAUSE + 1)
                else:
                    with act.Fori(1, NB) as ib:
                        body(ib)

            prepare(0)
            for m in range(2 * B):
                attend(m, follows=m > 0)
            copy_out(2 * B - 1, NB - 1)
            for batch_jobs in LAST:
                for l, b, j, q in batch_jobs:
                    lane_copy(l, j)
                for l, b, j, q in batch_jobs:
                    lane_store(l, "ffn", b, q, j)
            act.wait_ge(bn_ready, 1)
            shift = bn_mv[:, 5:6]
            for s in range(WARM + LEN):
                for g in range(NG):
                    gs = slice(g * GC, (g + 1) * GC)
                    dst = state(s)[:, gs]
                    act.wait_ge(z_ready[g], s + 1)
                    nc.scalar.activation(dst, z_buf[:, gs], ACT.Sigmoid, bias=shift).then_inc(y_ready[g], 1)
            act.wait_ge(flag_ready, 1)
            far = act.value_load(flag[0:1, 0:1], min_val=0, max_val=1)
            DONE = WARM + LEN
            with act.If(far > 0):
                with act.Fori(0, SEQ) as k:
                    for s in range(LEN):
                        act.wait_ge(z_ready[0], DONE + k * LEN + s + 1)
                        nc.scalar.activation(seq_cols(ys, s, k + 1), z_buf[:, 0:B].rearrange("p (b o) -> p b o", o=1),
                                             ACT.Sigmoid, bias=shift).then_inc(y_ready[0], 1)

        @block.vector
        def _(dve):
            dve.sem_inc(lo_ready, 1)
            dve.sem_inc(o_normed, 1)
            dve.sem_inc(query_split, 2)
            dve.sem_inc(act_done, 1)
            dve.sem_inc(key_split, 1)
            steps = [0]

            def link(ins):
                ins.then_inc(dve_step, 1)
                steps[0] += 1
                dve.wait_ge(dve_step, steps[0])

            def rsqrt(src, v, y, w, after_each):
                after_each(nc.vector.tensor_scalar(v, src, 1e-5, None, ALU.add))
                after_each(nc.vector.tensor_scalar(w.bitcast(I32), v.bitcast(I32), 1, None, ALU.logical_shift_right))
                after_each(nc.vector.tensor_scalar(y.bitcast(I32), w.bitcast(I32), -1.0, GUESS, ALU.mult, ALU.add))
                for _ in range(3):
                    after_each(nc.vector.tensor_tensor(w, y, y, ALU.mult))
                    after_each(nc.vector.scalar_tensor_tensor(out=w, in0=w, scalar=-0.5, in1=v, op0=ALU.mult,
                                                              op1=ALU.mult))
                    after_each(nc.vector.scalar_tensor_tensor(out=y, in0=w, scalar=1.5, in1=y, op0=ALU.add,
                                                              op1=ALU.mult))

            def gn_count(b, q):
                nc.vector.bn_stats(gn_st[:, q, :], X[:, b * T + q * BLK:b * T + (q + 1) * BLK]).then_inc(gn_counted, 1)

            def gn_channels(b):
                dve.wait_ge(gn_counted, (b + 1) * NB)
                link(nc.vector.bn_aggr(gn_mv[:, :], gn_st[:, :, :].rearrange("p q s -> p (q s)")))
                mean, var = gn_mv[:, 0:1], gn_mv[:, 1:2]
                nc.vector.tensor_copy(gn_ms[:, 0:1], mean)
                link(nc.vector.tensor_tensor(gn_w[:, 2:3], mean, mean, ALU.mult))
                nc.vector.tensor_tensor(gn_ms[:, 1:2], var, gn_w[:, 2:3], ALU.add).then_inc(gn_sums, 1)

            def gn_scale(b):
                dve.wait_ge(gn_mean, b + 1)
                link(nc.vector.tensor_copy(gn_ms[:, :], small_bank[:, 0:2]))
                link(nc.vector.tensor_tensor(gn_w[:, 2:3], gn_ms[:, 0:1], gn_ms[:, 0:1], ALU.mult))
                link(nc.vector.tensor_tensor(gn_w[:, 0:1], gn_ms[:, 1:2], gn_w[:, 2:3], ALU.subtract))
                rsqrt(gn_w[:, 0:1], gn_w[:, 0:1], gn_w[:, 1:2], gn_w[:, 2:3], link)
                nc.vector.tensor_scalar(w_s[:, :, :].rearrange("p j c -> p (j c)"),
                                        w_t[:, 0:3, :].rearrange("p j c -> p (j c)"), gn_w[:, 1:2], None, ALU.mult)
                nc.vector.scalar_tensor_tensor(out=gn_w[:, 3:4], in0=gn_ms[:, 0:1], scalar=-1.0, in1=gn_w[:, 1:2],
                                               op0=ALU.mult, op1=ALU.mult).then_inc(gn_scaled, 1)

            def gn_bias(b):
                dve.wait_ge(gn_shift, b + 1)
                link(nc.vector.tensor_tensor(bias_s[:, 0:2], bias12[:, :], small_bank[:, 0:2], ALU.add))
                nc.vector.tensor_scalar(bias_s[:, 2:4], bias_s[:, 0:2], -1.0, None, ALU.mult)
                nc.vector.tensor_tensor(ba_s, ba_row[0:1, :], small_bank[0:1, 128:256], ALU.add) \
                    .then_inc(gn_done, 1)

            def prepare(b):
                s = b % 2
                gn_bias(b)
                if b:
                    done = ((b - 1) * NB + PAUSE) * 16
                    dve.wait_ge(sum_added, done + 1)
                    dve.wait_ge(lo_ready, done + 1)
                with dve.Fori(0, NB // 2) as i:
                    for h in range(2):
                        n = b * NB + 2 * i + h
                        q = blk(2 * i + h)
                        dve.wait_ge(relu_done, n + 2)
                        for j in range(3):
                            last = nc.vector.scalar_tensor_tensor(out=pos[h][j], in0=neg[j], scalar=neg_a[:, j:j + 1],
                                                                  in1=pos[h][j], op0=ALU.mult, op1=ALU.add)
                        last.then_inc(act_done, 1)
                        dve.wait_ge(act_done, n + 2)
                        dve.wait_ge(key_split, n + 1)
                        key = pos[h][1]
                        nc.vector.tensor_copy(key_a[s][0:CH, q], key[0:CH, :])
                        nc.vector.tensor_copy(hi_tmp[CH:C, :], key[CH:C, :]).then_inc(key_copied, 1)
                        dve.wait_ge(key_copied, n + 1)
                        nc.vector.tensor_tensor(key_a[s][CH:C, q], key[CH:C, :], hi_tmp[CH:C, :], ALU.subtract) \
                            .then_inc(key_split, 1)
                    for h in range(2):
                        n = b * NB + 2 * i + h
                        q = blk(2 * i + h)
                        dve.wait_ge(query_copied, n + 1)
                        nc.vector.tensor_tensor(query_b[s][0:CH, q], pos[h][0][0:CH, :], query_a[s][0:CH, q],
                                                ALU.subtract).then_inc(query_split, 1)

            def reduce_max(b, ib, p):
                v = b * 128 + ib * 16 + p
                if p == 0:
                    dve.wait_ge(max_found, b * NB + ib)
                dve.wait_ge(mx_ready, v + 1)
                nc.vector.reduce_max(part_max[:, p:p + 1], mx_bank, AX.X).then_inc(mx_read, 1)

            def find_max(g):
                dve.wait_ge(mx_read, (g + 1) * 16)
                dve.wait_ge(max_turned, g)
                nc.vector.tensor_reduce(tile_max, part_max.rearrange("p (t k) -> p t k", k=4),
                                        AX.X, ALU.max).then_inc(max_found, 1)

            def split_max(g):
                dve.wait_ge(max_turned, g + 1)
                dve.wait_ge(m_moved, 32 * g)
                turned = small_bank[0:4, 0:128]
                nc.vector.tensor_scalar(m_hi, turned, -1.0 / MROW, None, ALU.mult).then_inc(m_hi_made, 1)
                dve.wait_ge(m_hi_made, g + 1)
                nc.vector.scalar_tensor_tensor(out=m_lo, in0=turned, scalar=-1.0 / MROW, in1=m_hi,
                                               op0=ALU.mult, op1=ALU.subtract).then_inc(m_ready, 1)

            dve.wait_ge(x_loaded[0], 16)
            for q in range(NB):
                gn_count(0, q)
            gn_channels(0)
            dve.wait_ge(w_ready, 1)
            gn_scale(0)
            dve.wait_ge(alpha_ready, 1)

            def invert(m, ib):
                dve.wait_ge(sums_ready, m * NB + ib + 1)
                nc.vector.reciprocal(inv_sum[:, :], small_bank[:, 0:4]).then_inc(inv_ready, 1)

            def copy_rows(m, ib):
                dve.wait_ge(inv_turned, m * NB + ib + 1)
                nc.vector.tensor_copy(inv_rows[:, :], small_bank[0:4, 0:128]).then_inc(rows_ready, 1)

            def normalise(m, ib):
                nb = m * NB + ib
                dve.wait_ge(inv_spread, nb + 1)
                dve.wait_ge(o_copied, nb + 1)
                dve.wait_ge(x_updated, nb)
                nc.vector.tensor_tensor(o_norm, o_copy, small_bank, ALU.mult).then_inc(o_normed, 1)

            def lane_stats(l, j, done):
                dve.wait_ge(lane_turned[l], j + 1)
                for t in range(4):
                    last = nc.vector.bn_stats(lane_st[:, 4 * l + t, :], bank(lane_bank[l])[:, t * 128:(t + 1) * 128])
                last.then_inc(lane_step[l], 1)
                dve.wait_ge(lane_step[l], done + 1)
                nc.vector.tensor_copy(lane_w[:, 2, 4 * l:4 * l + 4], lane_st[:, 4 * l:4 * l + 4, 1])
                for t in range(4):
                    last = nc.vector.bn_aggr(lane_mv[:, 4 * l + t, :], lane_st[:, 4 * l + t, :])
                last.then_inc(lane_step[l], 1)
                dve.wait_ge(lane_step[l], done + 2)

            def lane_rsqrt(l, j):
                done = [2]

                def after_each(ins):
                    ins.then_inc(lane_step[l], 1)
                    done[0] += 1
                    dve.wait_ge(lane_step[l], j * STEPS + done[0])

                mine = slice(4 * l, 4 * l + 4)
                rsqrt(lane_mv[:, mine, 1], lane_w[:, 0, mine], lane_w[:, 1, mine], lane_w[:, 2, mine], after_each)
                assert done[0] == STEPS

            def lane_norm(l, j):
                for t in range(4):
                    ts, k = slice(t * 128, (t + 1) * 128), 4 * l + t
                    last = nc.vector.tensor_scalar(lane_t[l][:, ts], bank(lane_bank[l])[:, ts], lane_mv[:, k, 0:1],
                                                   lane_w[:, 1, k:k + 1], ALU.subtract, ALU.mult)
                last.then_inc(lane_normed[l], 1)

            def lane_lo(l, b, q, j):
                dve.wait_ge(t_hi_ready, j + 1)
                nc.vector.tensor_tensor(t_lo[b % 2][:, blk(q)], lane_t[l], t_hi[b % 2][:, blk(q)], ALU.subtract) \
                    .then_inc(t_lo_ready, 1)

            def lane_count(l, b, q, j):
                dve.wait_ge(lane_stored[l], j + 1)
                nc.vector.bn_stats(bn_st[:, bass.ds(b * NB + q, 1), :], wx[:, wx_cols(b, q)]).then_inc(wx_counted, 1)

            def attend(m, follows):
                def body(ib):
                    has_before = follows or not isinstance(ib, int) or ib > 0
                    chained = m < B - 1 or m == B - 1 and not (isinstance(ib, int) and ib == NB - 1)
                    norms_next = m + 1 < B and isinstance(ib, int) and ib == 0
                    for p in range(NP):
                        n = m * 128 + ib * 16 + p
                        unit = max_unit(m, ib, p)
                        if unit:
                            reduce_max(*unit)
                        if p == 7 and chained:
                            find_max(m * NB + ib + 1)
                        dve.wait_ge(full_ready, n + 2)
                        dve.wait_ge(pv_done, n + 2)
                        nc.vector.tensor_tensor(p_lo[p % 2], p_full[p % 2], p_hi[p % 4], ALU.subtract) \
                            .then_inc(lo_ready, 1)
                        if has_before:
                            if p == 5:
                                invert(*before(m, ib))
                            if p == 7:
                                copy_rows(*before(m, ib))
                            if p == 9:
                                normalise(*before(m, ib))
                        for l, kind, b, j0 in jobs(m):
                            j = j0 + ib
                            if p == 2 + l:
                                lane_stats(l, j, j * STEPS)
                            if p == 3 + l:
                                lane_rsqrt(l, j)
                                lane_norm(l, j)
                            if p == 6 and kind == "tokens":
                                lane_lo(l, b, ib, j)
                            if p == 15 and kind == "ffn":
                                lane_count(l, b, ib, j)
                        if p == 12 and chained:
                            split_max(m * NB + ib + 1)
                        if norms_next:
                            if p == 2:
                                dve.wait_ge(x_loaded[m + 1], 16)
                            if 2 <= p < 2 + NB:
                                gn_count(m + 1, p - 2)
                            if p == 13:
                                gn_channels(m + 1)
                            if p == NP - 1:
                                gn_scale(m + 1)

                body(0)
                if m < B:
                    with dve.Fori(1, PAUSE) as ib:
                        body(ib)
                    if m + 1 < B:
                        prepare(m + 1)
                    body(PAUSE)
                    body(PAUSE + 1)
                else:
                    with dve.Fori(1, NB) as ib:
                        body(ib)

            def finish(m):
                invert(m, NB - 1)
                copy_rows(m, NB - 1)
                normalise(m, NB - 1)

            prepare(0)
            for v in range(LEAD):
                if v == 16:
                    find_max(0)
                reduce_max(0, v // 16, v % 16)
                if v == 17:
                    split_max(0)
            for m in range(2 * B):
                attend(m, follows=m > 0)
            finish(2 * B - 1)
            for r, batch_jobs in enumerate(LAST):
                for l, b, j, q in batch_jobs:
                    lane_stats(l, j, (j - r) * STEPS + 2 * r)
                link(nc.vector.tensor_copy(lane_w[:, 0, :], lane_mv[:, :, 1]))
                rsqrt(lane_w[:, 0, :], lane_w[:, 0, :], lane_w[:, 1, :], lane_w[:, 2, :], link)
                for l, b, j, q in batch_jobs:
                    lane_norm(l, j)
                for l, b, j, q in batch_jobs:
                    lane_count(l, b, q, j)

            dve.wait_ge(wx_counted, B * NB)
            link(nc.vector.bn_aggr(bn_mv[:, 0:2], bn_st[:, :, :].rearrange("p j s -> p (j s)")))
            rsqrt(bn_mv[:, 1:2], bn_mv[:, 7:8], bn_mv[:, 3:4], bn_mv[:, 8:9], link)
            link(nc.vector.tensor_tensor(bn_mv[:, 4:5], bn_mv[:, 3:4], gb[:, 0:1], ALU.mult))
            link(nc.vector.tensor_tensor(bn_mv[:, 6:7], bn_mv[:, 0:1], bn_mv[:, 4:5], ALU.mult))
            nc.vector.tensor_tensor(bn_mv[:, 5:6], gb[:, 1:2], bn_mv[:, 6:7], ALU.subtract).then_inc(bn_ready, 1)
            dve.wait_ge(bn_ready, 1)
            gain = bn_mv[:, 4:5]

            def batch_cols(g, s):
                if s >= WARM:
                    return wx_steps[:, g * GC:(g + 1) * GC, s - WARM], 0
                return wx_steps[:, g * GC:(g + 1) * GC - 1, LEN - WARM + s], 1

            for s in range(WARM + LEN):
                for g in range(NG):
                    src, skip = batch_cols(g, s)
                    z = z_buf[:, g * GC + skip:(g + 1) * GC]
                    if s == 0:
                        if g == 0:
                            link(nc.vector.memset(z_buf, 0.0))
                        nc.vector.tensor_scalar(z, src, gain, None, ALU.mult).then_inc(z_ready[g], 1)
                    else:
                        dve.wait_ge(vy_ready[g], s)
                        nc.vector.scalar_tensor_tensor(out=z, in0=src, scalar=gain,
                                                       in1=bank(g)[:, skip:GC], op0=ALU.mult,
                                                       op1=ALU.add).then_inc(z_ready[g], 1)
                if s == WARM - 1:
                    for g in range(NG):
                        dve.wait_ge(y_ready[g], WARM)
                    nc.vector.memset(y_began.rearrange("p (b k) -> p b k", b=B)[:, :, 0:1], 0.0) \
                        .then_inc(start_set, 1)
            for g in range(NG):
                dve.wait_ge(y_ready[g], WARM + LEN)
            dve.wait_ge(start_set, 1)
            began = y_began.rearrange("p (b k) -> p b k", b=B)[:, :, 1:CHUNKS]
            ended = ys[:, LEN - 1, :].rearrange("p (b k) -> p b k", b=B)[:, :, 0:CHUNKS - 1]
            diff = z_buf[:, 0:B * (CHUNKS - 1)].rearrange("p (b k) -> p b k", b=B)
            link(nc.vector.tensor_tensor(diff, began, ended, ALU.subtract))
            link(nc.vector.tensor_tensor(diff, diff, diff, ALU.mult))
            link(nc.vector.tensor_scalar(diff, diff, CLOSE * CLOSE, None, ALU.is_le))
            nc.vector.tensor_reduce(gap[:, 0:1], diff, AX.XY, ALU.min).then_inc(gap_ready, 1)
            dve.wait_ge(gap_max, 1)
            link(nc.vector.tensor_reduce(gap[0:1, 1:2], small_bank[0:1, 0:128], AX.X, ALU.min))
            nc.vector.tensor_scalar(flag[0:1, 0:1], gap[0:1, 1:2], -1.0, 1.0, ALU.mult, ALU.add) \
                .then_inc(flag_ready, 1)
            dve.wait_ge(flag_ready, 1)
            far = dve.value_load(flag[0:1, 0:1], min_val=0, max_val=1)
            DONE = WARM + LEN
            with dve.If(far > 0):
                with dve.Fori(0, SEQ) as k:
                    for s in range(LEN):
                        dve.wait_ge(vy_ready[0], DONE - 1 + k * LEN + s + 1)
                        src = wx_steps[:, :, s].rearrange("p (b k) -> p b k", b=B)[:, :, bass.ds(k + 1, 1)]
                        nc.vector.scalar_tensor_tensor(
                            out=z_buf[:, 0:B].rearrange("p (b o) -> p b o", o=1), in0=src, scalar=gain,
                            in1=bank(0)[:, 0:B].rearrange("p (b o) -> p b o", o=1),
                            op0=ALU.mult, op1=ALU.add).then_inc(z_ready[0], 1)
                dve.wait_ge(y_ready[0], DONE + SEQ * LEN)
            for b in range(B):
                x_b = X[:, b * T:(b + 1) * T].rearrange("p (k s) -> p k s", s=LEN)
                first = WX_SLOT[b] * CHUNKS
                y_b = ys[:, :, first:first + CHUNKS].rearrange("p s k -> p k s")
                nc.vector.tensor_tensor(x_b, x_b, y_b, ALU.add).then_inc(out_ready, 1)

        @block.gpsimd
        def _(pool):
            pool.sem_inc(sum_added, 1)
            pool.sem_inc(value_split, 2)
            made = [0]

            def link(ins):
                ins.then_inc(pool_step, 1)
                made[0] += 1
                pool.wait_ge(pool_step, made[0])

            nc.gpsimd.memset(ones[:, :], 1.0)
            nc.gpsimd.memset(zero[:, :], 0.0)
            nc.gpsimd.memset(lift[:, 0:1], LIFT)
            nc.gpsimd.memset(lift[:, 1:2], LIFT - ROWMAX)
            nc.gpsimd.memset(ident[:, :], 0.0)
            link(nc.gpsimd.memset(group_mean[:, :], 1.0 / GROUP))
            for s in range(2):
                link(nc.gpsimd.memset(key_b[s][CH:CH + 2, :], MROW))
            nc.gpsimd.affine_select(out=ident[:, :], in_=ident[:, :], compare_op=ALU.not_equal, fill=1.0,
                                    base=0, pattern=[[-1, C]], channel_multiplier=1)
            gm = group_mean[:, :].rearrange("p (g r) -> p g r", r=GROUP)
            link(nc.gpsimd.affine_select(out=gm, in_=gm, compare_op=ALU.is_ge, fill=0.0, base=0,
                                         pattern=[[-GROUP, C // GROUP], [0, GROUP]], channel_multiplier=1))
            link(nc.gpsimd.affine_select(out=gm, in_=gm, compare_op=ALU.is_ge, fill=0.0, base=GROUP - 1,
                                         pattern=[[GROUP, C // GROUP], [0, GROUP]], channel_multiplier=-1))
            nc.gpsimd.tensor_copy(ident16[:, :], ident[:, :]).then_inc(consts_set, 1)

            def prepare(b):
                s = b % 2
                with pool.Fori(0, NB // 2) as i:
                    for h in range(2):
                        n = b * NB + 2 * i + h
                        q = blk(2 * i + h)
                        pool.wait_ge(act_done, n + 2)
                        nc.gpsimd.tensor_copy(value_hi[s][:, q], pos[h][2]).then_inc(value_copied, 1)
                        nc.gpsimd.tensor_copy(key_b[s][0:CH, q], pos[h][1][0:CH, :])
                        pool.wait_ge(value_copied, n + 1)
                        nc.gpsimd.tensor_tensor(value_lo[s][:, q], pos[h][2], value_hi[s][:, q], ALU.subtract) \
                            .then_inc(value_split, 1)

            def stage(l, b, q, j):
                pool.wait_ge(x_updated, ((B if l else 0) + b) * NB + q + 1)
                pool.wait_ge(lane_done[l], j)
                nc.gpsimd.tensor_copy(lane_x[l], X[:, cols(b, q)]).then_inc(lane_staged[l], 1)

            def update(m, ib):
                nb = m * NB + ib
                pool.wait_ge(o_normed, nb + 2)
                x_b = X[:, cols(m % B, ib)]
                nc.gpsimd.tensor_tensor(x_b, x_b, o_norm, ALU.add).then_inc(x_updated, 1)

            def attend(m, follows):
                def body(ib):
                    has_before = follows or not isinstance(ib, int) or ib > 0
                    for l, kind, b, j0 in jobs(m):
                        stage(l, b, ib, j0 + ib)
                    for p in range(NP):
                        nb = m * NB + ib
                        n = nb * 16 + p
                        full = p_full[p % 2]
                        pool.wait_ge(full_ready, n + 2)
                        pool.wait_ge(sum_added, n + 1)
                        if p == 0:
                            last = nc.gpsimd.tensor_tensor(sum_run, full, zero[:, 0:1].broadcast_to([C, 1024]), ALU.add)
                        elif p < NP - 1:
                            last = nc.gpsimd.tensor_tensor(sum_run, sum_run, full, ALU.add)
                        else:
                            pool.wait_ge(sums_ready, nb)
                            last = nc.gpsimd.tensor_tensor(sum_end, sum_run, full, ALU.add)
                        last.then_inc(sum_added, 1)
                        if p == 10 and has_before:
                            update(*before(m, ib))

                body(0)
                if m < B:
                    with pool.Fori(1, PAUSE) as ib:
                        body(ib)
                    if m + 1 < B:
                        prepare(m + 1)
                    body(PAUSE)
                    body(PAUSE + 1)
                else:
                    with pool.Fori(1, NB) as ib:
                        body(ib)

            prepare(0)
            for m in range(2 * B):
                attend(m, follows=m > 0)
            update(2 * B - 1, NB - 1)


_INS = ['x', 'L0_conv_w1', 'L0_conv_b1', 'L0_conv_a1', 'L0_conv_w2', 'L0_conv_b2', 'L0_conv_a2', 'L0_conv_wa',
        'L0_conv_ba', 'L0_conv_aa', 'L1_ffn_W', 'L1_ffn_V', 'L1_ffn_gamma', 'L1_ffn_beta']


def kernel(**inputs):
    import numpy as _np
    import concourse.bacc as _bacc
    from concourse import mybir as _mybir
    from concourse.bass_utils import run_bass_kernel_spmd as _run

    nc = _bacc.Bacc("TRN2", target_bir_lowering=False, num_devices=1)
    n, c, h, w = inputs["x"].shape
    shapes = {"x": (n, c, h * w), "L0_conv_ba": (1, c)}
    arrays, args = {}, []
    for name in _INS:
        a = _np.ascontiguousarray(inputs[name])
        if name in shapes:
            a = a.reshape(shapes[name])
        elif a.ndim < 2:
            a = a.reshape(-1, 1)
        arrays[f"in_{name}"] = a
        args.append(nc.dram_tensor(f"in_{name}", a.shape, _mybir.dt.from_np(a.dtype), kind="ExternalInput").ap())
    args.append(nc.dram_tensor("out_0", (n, c, h * w), _mybir.dt.float32, kind="ExternalOutput").ap())
    hybrid_kernel(nc, *args)
    r = _run(nc, [arrays], core_ids=[0])
    return r.results[0]["out_0"].reshape(n, c, h, w)
```

```python
import concourse.bass as bass
from concourse import mybir
from contextlib import ExitStack
from math import log

F32 = mybir.dt.float32
F16 = mybir.dt.float16
I32 = mybir.dt.int32
ACT = mybir.ActivationFunctionType
ALU = mybir.AluOpType
AX = mybir.AxisListType


def hybrid_kernel(nc, x, w1, b1, a1, w2, b2, a2, wa, ba, aa, W, V, gamma, beta, out):
    B, C, T = x.shape
    CH = w1.shape[0]
    BLK = 512
    NB = T // BLK
    NP = T // 256
    GROUP = C // 32
    HALF = BLK // 2
    LIFT = 6.0 * log(2.0)
    INV = 2.0 ** 16
    MROW = 64.0
    ROWMAX = float(C) ** 0.5
    LEN = 16
    CHUNKS = T // LEN
    WARM = 12
    COLS = B * CHUNKS
    NG = 4
    GC = COLS // NG
    CLOSE = 2.0 ** -18
    assert C == 128 and CH == 64 and T == 4096 and B == 4 and CHUNKS == COLS // NG

    with ExitStack() as ctx:
        def sb(name, shape, dt=F32):
            return ctx.enter_context(nc.sbuf_tensor(name, shape, dt))

        def signal(name):
            return ctx.enter_context(nc.semaphore(name))

        X = sb("X", [C, B * T])
        REG = sb("REG", [C, 32768])
        scratch = sb("scratch", [C, 4, BLK])

        def f32(at, n):
            return REG[:, at:at + n]

        def f16(at, n):
            return REG[:, at:at + n // 2].bitcast(F16)

        SET = 12288
        key_a = [f16(s * SET, T) for s in range(2)]
        key_b = [f16(s * SET + 2048, T) for s in range(2)]
        query_a = [f16(s * SET + 4096, T) for s in range(2)]
        query_b = [f16(s * SET + 6144, T) for s in range(2)]
        value_hi = [f16(s * SET + 8192, T) for s in range(2)]
        value_lo = [f16(s * SET + 10240, T) for s in range(2)]
        u_hi = [f16(0, T), f16(16384, T)]
        u_lo = [f16(2048, T), f16(18432, T)]
        t_hi = [f16(8192, T), f16(20480, T)]
        t_lo = [f16(10240, T), f16(22528, T)]
        WORK = 2 * SET
        p_hi = [f16(WORK + 512 * j, 1024) for j in range(4)]
        p_lo = [f16(WORK + 2048 + 512 * j, 1024) for j in range(2)]
        p_full = [f32(WORK + 3072 + 1024 * j, 1024) for j in range(2)]
        sum_run, sum_end = f32(WORK + 5120, 1024), f32(WORK + 6144, BLK)
        o_copy, o_norm = f32(WORK + 7168, BLK), f32(WORK + 7680, BLK)
        prelu = [[f32(WORK + 1536 * h + 512 * j, BLK) for j in range(3)] for h in range(2)]
        neg = [[f32(WORK + 3072 + 512 * j, BLK) for j in range(3)],
               [scratch[:, 0, :], scratch[:, 2, :], f32(WORK + 6656, BLK)]]
        hi_tmp = f16(WORK + 4608, BLK)
        WX_SLOT = [1, 3, 0, 2]
        wx = f32(0, B * T)
        ys = f32(B * T, B * T).rearrange("p (s c) -> p s c", c=COLS)

        w_t = sb("w_t", [C, 5, C])
        w_in = f32(WORK + 5120, 5 * C).rearrange("p (j c) -> p j c", c=C)
        w1_t, w2_t, wa_t, W_t, V_t = [w_t[:, j, :] for j in range(5)]
        ident = sb("ident", [C, C])
        ident16 = sb("ident16", [C, C], F16)
        group_mean = sb("group_mean", [C, C])
        ones = sb("ones", [C, C])
        zero = sb("zero", [C, 1])
        ba_row = sb("ba_row", [1, C])
        a_row = sb("a_row", [1, 4])
        bias12 = sb("bias12", [C, 2])
        one_less_a = sb("one_less_a", [C, 4])
        lift = sb("lift", [C, 2])
        gb = sb("gb", [C, 2])
        gn_st = sb("gn_st", [C, NB, 6])
        gn_mv = sb("gn_mv", [C, 2])
        gn_ms = sb("gn_ms", [C, 2])
        gn_w = sb("gn_w", [C, 5])
        w_s = scratch[:, 1, 0:3 * C].rearrange("p (j c) -> p j c", c=C)
        bias_s = sb("bias_s", [C, 4])
        ba_s = scratch[0:1, 1, 3 * C:4 * C]
        lane_st = sb("lane_st", [C, 8, 6])
        lane_mv = sb("lane_mv", [C, 8, 2])
        lane_w = sb("lane_w", [C, 3, 8])
        bn_st = sb("bn_st", [C, B * NB, 6])
        bn_mv = sb("bn_mv", [C, 10])
        part_max = scratch[:, 3, 0:16]
        tile_max = scratch[:, 3, 16:20]
        m_hi = scratch[0:4, 3, 64:128].bitcast(F16)
        m_lo = scratch[0:4, 3, 128:192].bitcast(F16)
        inv_sum = scratch[:, 3, 20:24]
        inv_hi = scratch[0:4, 3, 192:256].bitcast(F16)
        inv_lo = scratch[0:4, 3, 256:320].bitcast(F16)
        lane_bank = (7, 6)
        lane_x = [scratch[:, 0, :], scratch[:, 1, :]]
        lane_t = [scratch[:, 2, :], scratch[:, 3, :]]
        y_began, z_buf = [scratch[:, 2 * j:2 * j + 2, :].rearrange("p a c -> p (a c)") for j in range(2)]
        gap = sb("gap", [C, 4])
        flag = sb("flag", [1, 1], I32)

        PS = ctx.enter_context(nc.psum_tensor("PS", [C, 8 * BLK], F32))

        def bank(j, n=1):
            return PS[:, j * BLK:(j + n) * BLK]

        o_bank, mx_bank, small_bank = bank(4), bank(5, 2), bank(7)
        proj_bank = [bank(j) for j in (0, 1, 2, 3, 5, 6)]

        x_loaded = [signal(f"x_loaded{b}") for b in range(B)]
        w_loaded = signal("w_loaded")
        consts_set = signal("consts_set")
        w_turned = signal("w_turned")
        w_ready = signal("w_ready")
        alpha_ready = signal("alpha_ready")
        dve_step = signal("dve_step")
        pool_step = signal("pool_step")
        gn_sums = signal("gn_sums")
        gn_mean = signal("gn_mean")
        gn_counted = signal("gn_counted")
        gn_scaled = signal("gn_scaled")
        gn_shift = signal("gn_shift")
        gn_done = signal("gn_done")
        proj_done = signal("proj_done")
        relu_done = signal("relu_done")
        act_done = signal("act_done")
        high_copied = signal("high_copied")
        key_split = signal("key_split")
        query_split = signal("query_split")
        value_copied = signal("value_copied")
        value_split = signal("value_split")
        mx_ready = signal("mx_ready")
        mx_read = signal("mx_read")
        max_found = signal("max_found")
        max_turned = signal("max_turned")
        m_hi_made = signal("m_hi_made")
        m_ready = signal("m_ready")
        m_moved = signal("m_moved")
        scores_ready = signal("scores_ready")
        hi_ready = signal("hi_ready")
        full_ready = signal("full_ready")
        lo_ready = signal("lo_ready")
        pv_done = signal("pv_done")
        sum_added = signal("sum_added")
        o_copied = signal("o_copied")
        sums_folded = signal("sums_folded")
        sums_ready = signal("sums_ready")
        inv_ready = signal("inv_ready")
        inv_turned = signal("inv_turned")
        inv_hi_made = signal("inv_hi_made")
        inv_split = signal("inv_split")
        inv_spread = signal("inv_spread")
        inv_made = signal("inv_made")
        o_normed = signal("o_normed")
        x_updated = signal("x_updated")
        lanes = range(2)
        lane_staged = [signal(f"lane_staged{l}") for l in lanes]
        lane_turned = [signal(f"lane_turned{l}") for l in lanes]
        lane_step = [signal(f"lane_step{l}") for l in lanes]
        rstd_ready = [signal(f"rstd_ready{l}") for l in lanes]
        lane_normed = [signal(f"lane_normed{l}") for l in lanes]
        lane_back = [signal(f"lane_back{l}") for l in lanes]
        lane_copied = [signal(f"lane_copied{l}") for l in lanes]
        lane_done = [signal(f"lane_done{l}") for l in lanes]
        lane_stored = [signal(f"lane_stored{l}") for l in lanes]
        t_hi_ready = signal("t_hi_ready")
        t_lo_ready = signal("t_lo_ready")
        wx_counted = signal("wx_counted")
        bn_ready = signal("bn_ready")
        vy_ready = [signal(f"vy_ready{g}") for g in range(NG)]
        z_ready = [signal(f"z_ready{g}") for g in range(NG)]
        y_ready = [signal(f"y_ready{g}") for g in range(NG)]
        start_set = signal("start_set")
        gap_ready = signal("gap_ready")
        gap_max = signal("gap_max")
        flag_ready = signal("flag_ready")
        states_final = signal("states_final")
        out_ready = signal("out_ready")
        last_ready = signal("last_ready")
        stored = signal("stored")

        block = ctx.enter_context(nc.Block())
        x_v = x.rearrange("b c t -> c b t")
        out_v = out.rearrange("b c t -> c b t")

        def cols(b, q):
            return bass.ds(b * T + q * BLK, BLK)

        def blk(q):
            return bass.ds(q * BLK, BLK)

        wx_steps = wx.rearrange("p (n s) -> p n s", s=LEN)
        GUESS = float(0x5f3759df)
        RSQRT = 12
        STEPS = RSQRT + 2

        LAG = 2

        def jobs(m, ib):
            found = []
            if B - 1 <= m < 2 * B - 1:
                found.append((0, "tokens", m - (B - 1), ib, (m - (B - 1)) * NB + ib))
            elif m == 2 * B - 1 and not (isinstance(ib, int) and ib < LAG):
                found.append((0, "ffn", B - 1, ib - LAG, B * NB + ib - LAG))
            if m > B:
                found.append((1, "ffn", m - B - 1, ib, (m - B - 1) * NB + ib))
            return found

        LAST = [(0, B - 1, NB - 2, B * NB + NB - LAG), (1, B - 1, NB - 1, (B - 1) * NB)]

        LEAD = 24
        PAUSE = NB - 2

        def lead_bank(v):
            return (mx_bank, bank(0, 2), bank(2, 2))[v % 3]

        def max_unit(m, ib, p):
            block, unit = (ib + 1, p + 8) if p < 8 else (ib + 2, p - 8)
            if isinstance(block, int) and block >= NB:
                m, block = m + 1, block - NB
            return (m, block, unit) if m < B else None

        def ffn_job(l, j):
            return j - B * NB if l == 0 else j

        def wx_cols(b, q):
            return bass.ds(WX_SLOT[b] * T + q * BLK, BLK)

        def after(m):
            return 6 if m < B else 7

        def before(m, ib):
            return (m, ib - 1) if not isinstance(ib, int) or ib else (m - 1, NB - 1)

        SEQ = CHUNKS - 1

        def state(s):
            if s >= WARM:
                return ys[:, s - WARM, :]
            return y_began if s == WARM - 1 else ys[:, LEN // 2 + s % 2, :]

        def last_sum(b, half):
            n = CHUNKS // 2
            first = WX_SLOT[b] * CHUNKS + half * n
            return (X[:, out_cols(b, half)].rearrange("p (k s) -> p k s", s=LEN),
                    ys[:, :, first:first + n].rearrange("p s k -> p k s"))

        def out_cols(b, half):
            return slice(b * T + half * T // 2, b * T + (half + 1) * T // 2)

        def seq_cols(buf, s, k):
            return buf[:, s, :].rearrange("p (b k) -> p b k", b=B)[:, :, bass.ds(k, 1)]

        @block.sync
        def _(sp):
            for b in range(B):
                sp.dma_start(X[:, b * T:(b + 1) * T], x[b]).then_inc(x_loaded[b], 16)
                if b == 0:
                    for half in range(2):
                        rows = slice(CH * half, CH * half + CH)
                        sp.dma_start(w_in[rows, 0, :], w1).then_inc(w_loaded, 16)
                        sp.dma_start(w_in[rows, 1, :], w2).then_inc(w_loaded, 16)
                        sp.dma_start(bias12[rows, 0:1], b1).then_inc(w_loaded, 16)
                        sp.dma_start(bias12[rows, 1:2], b2).then_inc(w_loaded, 16)
                    for j, w in enumerate((wa, W, V)):
                        sp.dma_start(w_in[:, 2 + j, :], w).then_inc(w_loaded, 16)
                    sp.dma_start(gb[:, 0:1], gamma).then_inc(w_loaded, 16)
                    sp.dma_start(gb[:, 1:2], beta).then_inc(w_loaded, 16)
                    sp.dma_start(ba_row[:, :], ba).then_inc(w_loaded, 16)
                    for j, a in enumerate((a1, a2, aa)):
                        sp.dma_start(a_row[0:1, j:j + 1], a).then_inc(w_loaded, 16)
            for b in range(B):
                with sp.Fori(0, NB) as ib:
                    for row, part in ((CH, m_hi), (CH + 1, m_lo)):
                        if row == CH:
                            sp.wait_ge(m_ready, b * NB + ib + 1)
                        sp.dma_start(query_b[b % 2][row:row + 1, blk(ib)].rearrange("o (t p) -> o t p", p=128),
                                     part).then_inc(m_moved, 16)
            for b, half in [(0, 0), (0, 1), (1, 0), (B - 1, 0), (1, 1), (2, 0), (2, 1), (B - 1, 1)]:
                if b < B - 1:
                    sp.wait_ge(out_ready, 2 * b + half + 1)
                else:
                    sp.wait_ge(last_ready, half + 1)
                sp.dma_start(out[b][:, half * T // 2:(half + 1) * T // 2], X[:, out_cols(b, half)]) \
                    .then_inc(stored, 16)
            sp.wait_ge(stored, 16 * 2 * B)

        W_LOADS = 16 * (8 + 3 + 3 + 3)

        @block.tensor
        def _(pe):
            pe.sem_inc(proj_done, 1)
            pe.sem_inc(pv_done, 3)

            pe.wait_ge(w_loaded, W_LOADS)
            pe.wait_ge(consts_set, 1)
            for j in range(5):
                last = nc.tensor.transpose(PS[:, j * C:(j + 1) * C], w_in[:, j, :], ident[:, :])
            last.then_inc(w_turned, 1)
            nc.tensor.matmul(small_bank[:, 0:3], ones[0:1, :], a_row[0:1, 0:3], start=True, stop=True) \
                .then_inc(w_turned, 1)
            pe.wait_ge(w_ready, 1)
            pe.wait_ge(alpha_ready, 1)

            def gn_group(b):
                if b:
                    nb = (b - 1) * NB + PAUSE - 1
                    pe.wait_ge(m_ready, nb + 1)
                    pe.wait_ge(o_normed, nb)
                pe.wait_ge(gn_sums, b + 1)
                nc.tensor.matmul(small_bank[:, 0:2], group_mean[:, :], gn_ms[:, :], start=True, stop=True) \
                    .then_inc(gn_mean, 1)

            def gn_biases(b):
                if b:
                    pe.wait_ge(m_ready, (b - 1) * NB + PAUSE + 1)
                pe.wait_ge(gn_scaled, b + 1)
                shift = gn_w[:, 3:4]
                nc.tensor.matmul(small_bank[:, 0:1], w1_t, shift, start=True, stop=True)
                nc.tensor.matmul(small_bank[:, 1:2], w2_t, shift, start=True, stop=True)
                nc.tensor.matmul(small_bank[0:1, 128:256], shift, wa_t, start=True, stop=True).then_inc(gn_shift, 1)

            def prepare(b):
                pe.wait_ge(gn_done, b + 1)
                if b:
                    done = ((b - 1) * NB + PAUSE) * 16
                    pe.wait_ge(full_ready, done + 1)
                    pe.wait_ge(mx_read, done + LEAD)
                for q in range(NB):
                    h, x_q = q % 2, X[:, b * T + q * BLK:b * T + (q + 1) * BLK]
                    pe.wait_ge(act_done, b * NB + q)
                    nc.tensor.matmul(proj_bank[3 * h], w_s[:, 0, :], x_q, start=True, stop=True) \
                        .then_inc(proj_done, 1)
                    nc.tensor.matmul(proj_bank[3 * h + 1], w_s[:, 1, :], x_q, start=True, stop=True) \
                        .then_inc(proj_done, 1)
                    for t in range(4):
                        o = proj_bank[3 * h + 2][:, t * C:(t + 1) * C]
                        nc.tensor.matmul(o, x_q[:, t * 128:(t + 1) * 128], w_s[:, 2, :], start=True, stop=False)
                        last = nc.tensor.matmul(o, ones[0:1, :], ba_s, start=False, stop=True)
                    last.then_inc(proj_done, 1)
                if b:
                    pe.wait_ge(act_done, (b + 1) * NB)
                else:
                    pe.wait_ge(query_split, NB + 2)

            def max_scores(b, ib, p, held=1):
                v = b * 128 + ib * 16 + p
                dst = mx_bank if held == 1 else lead_bank(v)
                if held == 1 or v >= held:
                    pe.wait_ge(mx_read, v - held + 1)
                for t in range(2):
                    last = nc.tensor.matmul(dst[:, t * BLK:(t + 1) * BLK],
                                            query_a[b % 2][:, bass.ds(ib * BLK + p // 4 * 128, 128)],
                                            key_a[b % 2][:, (p % 4 * 2 + t) * BLK:(p % 4 * 2 + t + 1) * BLK],
                                            start=True, stop=True)
                last.then_inc(mx_ready, 1)

            def turn_max(g):
                pe.wait_ge(max_found, g + 1)
                nc.tensor.transpose(small_bank[0:4, 0:128], tile_max, ident[:, :]).then_inc(max_turned, 1)

            def products(m):
                s = m % 2
                if m < B:
                    return [(key_a[s], query_a[s], C), (key_b[s], query_b[s], CH + 2)], value_hi[s], value_lo[s]
                return [(u_hi[s], u_hi[s], C), (u_hi[s], u_lo[s], C), (u_lo[s], u_hi[s], C)], t_hi[s], t_lo[s]

            def scores(m, ib, p):
                n = m * 128 + ib * 16 + p
                score_terms = products(m)[0]
                if m < B and p == 0:
                    pe.wait_ge(m_moved, 32 * (m * NB + ib + 1))
                pe.wait_ge(full_ready, n)
                for t in range(2):
                    j = 2 * p + t
                    for k, (key, query, rows) in enumerate(score_terms):
                        last = nc.tensor.matmul(bank(p % 2 * 2 + t), key[0:rows, j * 128:(j + 1) * 128],
                                                query[0:rows, blk(ib)], start=(k == 0),
                                                stop=(k == len(score_terms) - 1))
                last.then_inc(scores_ready, 1)

            def weigh(m, ib, p):
                n = m * 128 + ib * 16 + p
                v_hi, v_lo = products(m)[1:]
                pe.wait_ge(hi_ready, n + 1)
                if p == 0:
                    pe.wait_ge(o_copied, m * NB + ib)
                for v in (v_hi, v_lo):
                    for t in range(2):
                        j = 2 * p + t
                        nc.tensor.matmul(o_bank, v[:, j * 128:(j + 1) * 128], p_hi[p % 4][:, t * BLK:(t + 1) * BLK],
                                         start=(p == 0 and t == 0 and v is v_hi), stop=False)
                pe.wait_ge(lo_ready, n + 2)
                for t in range(2):
                    j = 2 * p + t
                    last = nc.tensor.matmul(o_bank, v_hi[:, j * 128:(j + 1) * 128],
                                            p_lo[p % 2][:, t * BLK:(t + 1) * BLK],
                                            start=False, stop=(p == NP - 1 and t == 1))
                last.then_inc(pv_done, 1)

            def column_sums(m, ib, others=()):
                nb = m * NB + ib
                pe.wait_ge(sums_folded, nb + 1)
                pe.wait_ge(o_normed, nb + 1)
                for sem, events in others:
                    pe.wait_ge(sem, events)
                if m < B:
                    for t in range(4):
                        last = nc.tensor.matmul(small_bank[:, t:t + 1], sum_end[:, t * 128:(t + 1) * 128],
                                                ones[:, 0:1], start=True, stop=True)
                else:
                    last = nc.tensor.matmul(small_bank, ones[:, :], sum_end, start=True, stop=True)
                last.then_inc(sums_ready, 1)

            def turn_inverse(m, ib):
                pe.wait_ge(inv_ready, m * NB + ib + 1)
                nc.tensor.transpose(small_bank[0:4, 0:128], inv_sum, ident[:, :]).then_inc(inv_turned, 1)

            def spread_inverse(m, ib):
                pe.wait_ge(inv_split, m * NB + ib + 1)
                for t in range(4):
                    for part in (inv_hi, inv_lo):
                        last = nc.tensor.matmul(small_bank[:, t * 128:(t + 1) * 128],
                                                ident16[0:4, t:t + 1].broadcast_to([4, C]), part,
                                                start=part is inv_hi, stop=part is inv_lo)
                last.then_inc(inv_spread, 1)

            def lane_turn(l, x_q, j, staged):
                if staged:
                    pe.wait_ge(lane_staged[l], j + 1)
                pe.wait_ge(lane_stored[l], j)
                for t in range(4):
                    last = nc.tensor.transpose(bank(lane_bank[l])[:, t * 128:(t + 1) * 128],
                                               x_q[:, t * 128:(t + 1) * 128], ident[:, :])
                last.then_inc(lane_turned[l], 1)

            def lane_return(l, j):
                pe.wait_ge(lane_normed[l], j + 1)
                for t in range(4):
                    last = nc.tensor.transpose(bank(lane_bank[l])[:, t * 128:(t + 1) * 128],
                                               lane_t[l][:, t * 128:(t + 1) * 128], ident[:, :])
                last.then_inc(lane_back[l], 1)

            def lane_product(l, kind, b, q, j):
                if kind == "tokens":
                    pe.wait_ge(t_lo_ready, j + 1)
                    turned = bank(lane_bank[l]).bitcast(F16)
                    for part, src in enumerate((t_hi, t_lo)):
                        for t in range(4):
                            last = nc.tensor.transpose(turned[:, part * BLK + t * 128:part * BLK + (t + 1) * 128],
                                                       src[b % 2][:, bass.ds(q * BLK + t * 128, 128)],
                                                       ident16[:, :])
                else:
                    pe.wait_ge(lane_copied[l], ffn_job(l, j) + 1)
                    last = nc.tensor.matmul(bank(lane_bank[l]), W_t, lane_x[l], start=True, stop=True)
                last.then_inc(lane_done[l], 1)

            def attend(m, follows):
                def body(ib):
                    has_before = follows or not isinstance(ib, int) or ib > 0
                    resumes = m + 1 < B and isinstance(ib, int) and ib == PAUSE
                    pm, pb = before(m, ib)
                    nb = m * NB + ib
                    chained = m < B - 1 or m == B - 1 and not (isinstance(ib, int) and ib == NB - 1)
                    others = []
                    norms_next = m + 1 < B and isinstance(ib, int) and ib == PAUSE - 1
                    if norms_next:
                        others.append((gn_scaled, m + 2))
                    for l, kind, b, q, j in jobs(m, ib):
                        if l == 0:
                            others.append((lane_normed[l], j + 1))
                    for p in range(NP):
                        scores(m, ib, p)
                        if resumes and p == 0:
                            pe.wait_ge(act_done, (m + 2) * NB + 1)
                        if resumes and p == 8:
                            pe.wait_ge(query_split, (m + 2) * NB + 2)
                            pe.wait_ge(value_split, (m + 2) * NB + 2)
                        unit = max_unit(m, ib, p)
                        if unit:
                            max_scores(*unit)
                        if p >= 2:
                            weigh(m, ib, p - 2)
                        elif has_before and not resumes:
                            weigh(pm, pb, NP + p - 2)
                        if has_before:
                            if p == after(m):
                                column_sums(pm, pb, others)
                            if p == after(m) + 2 and pm < B:
                                turn_inverse(pm, pb)
                            if p == after(m) + 4 and pm < B:
                                spread_inverse(pm, pb)
                        if p == 12 and chained:
                            pe.wait_ge(o_normed, nb + 1)
                            turn_max(nb + 1)
                        for l, kind, b, q, j in jobs(m, ib):
                            if p == 1 + 7 * l:
                                lane_turn(l, lane_x[l], j, True)
                            if p == 13 and kind == "ffn":
                                if l == 0:
                                    pe.wait_ge(o_normed, nb + 1)
                                lane_return(l, j)
                            if p == 15:
                                if kind == "tokens":
                                    pe.wait_ge(o_normed, nb + 1)
                                    if chained:
                                        pe.wait_ge(m_ready, nb + 2)
                                lane_product(l, kind, b, q, j)
                        if p == 2 and norms_next:
                            gn_group(m + 1)
                        if p == NP - 1 and norms_next:
                            gn_biases(m + 1)

                body(0)
                if m < B:
                    with pe.Fori(1, PAUSE - 1) as ib:
                        body(ib)
                    body(PAUSE - 1)
                    if m + 1 < B:
                        weigh(m, PAUSE - 1, NP - 2)
                        weigh(m, PAUSE - 1, NP - 1)
                        prepare(m + 1)
                    body(PAUSE)
                    body(PAUSE + 1)
                else:
                    first = LAG if m == 2 * B - 1 else 1
                    for ib in range(1, first):
                        body(ib)
                    with pe.Fori(first, NB) as ib:
                        body(ib)

            def finish(m):
                weigh(m, NB - 1, NP - 2)
                weigh(m, NB - 1, NP - 1)
                column_sums(m, NB - 1, [(lane_stored[0], B * NB + NB - LAG)])

            gn_group(0)
            gn_biases(0)
            prepare(0)
            for v in range(LEAD):
                max_scores(0, v // 16, v % 16, held=3)
                if v == 17:
                    turn_max(0)
            pe.wait_ge(mx_read, LEAD)
            pe.wait_ge(value_split, NB + 2)
            for m in range(2 * B):
                if m >= B:
                    pe.wait_ge(lane_stored[0], (m - B + 1) * NB)
                attend(m, follows=m > 0)
            finish(2 * B - 1)
            pe.wait_ge(x_updated, 2 * B * NB)
            for l, b, q, j in LAST:
                lane_turn(l, X[:, b * T + q * BLK:b * T + (q + 1) * BLK], j, False)
            for l, b, q, j in LAST:
                lane_return(l, j)
            for l, b, q, j in LAST:
                lane_product(l, "ffn", b, q, j)

            pe.wait_ge(bn_ready, 1)
            for s in range(1, WARM + LEN):
                for g in range(NG):
                    gs = slice(g * GC, (g + 1) * GC)
                    prev = state(s - 1)[:, gs]
                    pe.wait_ge(y_ready[g], s)
                    if s == WARM:
                        pe.wait_ge(start_set, 1)
                    nc.tensor.matmul(bank(g)[:, 0:GC], V_t, prev, start=True, stop=True) \
                        .then_inc(vy_ready[g], 1)
            pe.wait_ge(gap_ready, 1)
            nc.tensor.transpose(small_bank[0:1, 0:128], gap[:, 0:1], ident[:, :]).then_inc(gap_max, 1)
            pe.wait_ge(flag_ready, 1)
            far = pe.value_load(flag[0:1, 0:1], min_val=0, max_val=1)
            DONE = WARM + LEN
            with pe.If(far > 0):
                with pe.Fori(0, SEQ) as k:
                    for s in range(LEN):
                        prev = seq_cols(ys, (s - 1) % LEN, k + (1 if s else 0))
                        pe.wait_ge(y_ready[0], DONE + k * LEN + s)
                        nc.tensor.matmul(bank(0)[:, 0:B], V_t, prev, start=True, stop=True) \
                            .then_inc(vy_ready[0], 1)

        @block.scalar
        def _(act):
            act.sem_inc(relu_done, 1)
            act.sem_inc(full_ready, 1)
            act.wait_ge(w_turned, 1)
            nc.scalar.activation(w_t[:, :, :].rearrange("p j c -> p (j c)"), PS[:, 0:5 * C], ACT.Copy) \
                .then_inc(w_ready, 1)
            act.wait_ge(w_turned, 2)
            nc.scalar.activation(one_less_a[:, 0:3], small_bank[:, 0:3], ACT.Identity, scale=-1.0, bias=ones[:, 0:1]) \
                .then_inc(alpha_ready, 1)

            def prepare(b):
                s = b % 2
                act.wait_ge(gn_done, b + 1)
                if b:
                    done = ((b - 1) * NB + PAUSE) * 16
                    act.wait_ge(pv_done, done + 3)
                    act.wait_ge(lo_ready, done + 1)
                    act.wait_ge(sum_added, done + 1)
                else:
                    act.wait_ge(alpha_ready, 1)

                def copy_high(q, h):
                    n = b * NB + q
                    act.wait_ge(act_done, n + 2)
                    nc.scalar.activation(query_a[s][:, blk(q)], prelu[h][0], ACT.Identity, bias=bias_s[:, 0:1])
                    nc.scalar.activation(key_a[s][0:CH, blk(q)], prelu[h][1][0:CH, :], ACT.Identity,
                                         bias=bias_s[0:CH, 1:2])
                    act.wait_ge(key_split, n + 1)
                    nc.scalar.activation(hi_tmp[CH:C, :], prelu[h][1][CH:C, :], ACT.Identity,
                                         bias=bias_s[CH:C, 1:2]).then_inc(high_copied, 1)

                def pair(i):
                    for h in range(2):
                        q = 2 * i + h
                        n = b * NB + q
                        if not isinstance(n, int) or n:
                            act.wait_ge(act_done, n)
                        for j in range(3):
                            act.wait_ge(proj_done, 3 * n + j + 2)
                            last = nc.scalar.activation(neg[h][j], proj_bank[3 * h + j], ACT.Relu, scale=-1.0,
                                                        bias=bias_s[:, 2 + j:3 + j] if j < 2 else 0.0)
                        last.then_inc(relu_done, 1)
                        if not isinstance(q, int) or q:
                            copy_high(q - 1, 1 - h)

                pair(0)
                with act.Fori(1, NB // 2) as i:
                    pair(i)
                copy_high(NB - 1, 1)

            def lane_stage(l, kind, b, q, j):
                act.wait_ge(x_updated, ((B if kind == "ffn" else 0) + b) * NB + q + 1)
                act.wait_ge(lane_done[l], j)
                nc.scalar.activation(lane_x[l], X[:, cols(b, q)], ACT.Copy).then_inc(lane_staged[l], 1)

            def lane_norm(l, j):
                act.wait_ge(rstd_ready[l], j + 1)
                for t in range(4):
                    ts, k = slice(t * 128, (t + 1) * 128), 4 * l + t
                    last = nc.scalar.activation(lane_t[l][:, ts], bank(lane_bank[l])[:, ts], ACT.Identity,
                                                bias=lane_w[:, 2, k:k + 1], scale=lane_w[:, 1, k:k + 1])
                last.then_inc(lane_normed[l], 1)

            def lane_hi(l, b, q, j):
                act.wait_ge(lane_normed[l], j + 1)
                nc.scalar.activation(t_hi[b % 2][:, blk(q)], lane_t[l], ACT.Copy).then_inc(t_hi_ready, 1)

            def lane_copy(l, j):
                act.wait_ge(lane_back[l], ffn_job(l, j) + 1)
                nc.scalar.activation(lane_x[l], bank(lane_bank[l]), ACT.Copy).then_inc(lane_copied[l], 1)

            def lane_store(l, kind, b, q, j):
                act.wait_ge(lane_done[l], j + 1)
                if kind == "tokens":
                    turned = bank(lane_bank[l]).bitcast(F16)
                    nc.scalar.activation(u_hi[b % 2][:, blk(q)], turned[:, 0:BLK], ACT.Copy)
                    last = nc.scalar.activation(u_lo[b % 2][:, blk(q)], turned[:, BLK:2 * BLK], ACT.Copy)
                else:
                    last = nc.scalar.activation(wx[:, wx_cols(b, q)], bank(lane_bank[l]), ACT.Copy)
                last.then_inc(lane_stored[l], 1)

            def copy_out(m, ib):
                nb = m * NB + ib
                act.wait_ge(pv_done, (nb + 1) * 16 + 3)
                act.wait_ge(o_normed, nb + 1)
                nc.scalar.activation(o_copy, o_bank, ACT.Copy).then_inc(o_copied, 1)

            def attend(m, follows):
                scale = 1.0 if m < B else C ** -0.5
                bias = lift[:, 0:1] if m < B else lift[:, 1:2]

                def body(ib):
                    has_before = follows or not isinstance(ib, int) or ib > 0
                    resumes = m + 1 < B and isinstance(ib, int) and ib == PAUSE
                    for l, kind, b, q, j in jobs(m, ib):
                        if l == 0:
                            lane_stage(l, kind, b, q, j)
                    for p in range(NP):
                        n = m * 128 + ib * 16 + p
                        src = bank(p % 2 * 2, 2)
                        if resumes and p in (0, 3):
                            act.wait_ge(query_split, (m + 2) * NB + 1 + p // 3)
                            act.wait_ge(value_split, (m + 2) * NB + 1 + p // 3)
                        act.wait_ge(scores_ready, n + 1)
                        act.wait_ge(pv_done, n)
                        nc.scalar.activation(p_hi[p % 4], src, ACT.Exp, bias=bias, scale=scale) \
                            .then_inc(hi_ready, 1)
                        if resumes and p == 1:
                            act.wait_ge(key_split, (m + 2) * NB + 1)
                        act.wait_ge(lo_ready, n)
                        act.wait_ge(sum_added, n)
                        nc.scalar.activation(p_full[p % 2], src, ACT.Exp, bias=bias, scale=scale) \
                            .then_inc(full_ready, 1)
                        if p == 1 and has_before:
                            copy_out(*before(m, ib))
                        for l, kind, b, q, j in jobs(m, ib):
                            if l == 1 and p == 5:
                                lane_stage(l, kind, b, q, j)
                            if p == 5 + 7 * l:
                                lane_norm(l, j)
                            if p == 6 and kind == "tokens":
                                lane_hi(l, b, q, j)
                            if p == 13 and kind == "ffn":
                                lane_copy(l, j)
                            if p == 15:
                                lane_store(l, kind, b, q, j)

                body(0)
                if m < B:
                    with act.Fori(1, PAUSE - 1) as ib:
                        body(ib)
                    body(PAUSE - 1)
                    if m + 1 < B:
                        prepare(m + 1)
                    body(PAUSE)
                    body(PAUSE + 1)
                else:
                    first = LAG if m == 2 * B - 1 else 1
                    for ib in range(1, first):
                        body(ib)
                    with act.Fori(first, NB) as ib:
                        body(ib)

            prepare(0)
            for m in range(2 * B):
                attend(m, follows=m > 0)
            copy_out(2 * B - 1, NB - 1)
            for l, b, q, j in LAST:
                lane_norm(l, j)
            for l, b, q, j in LAST:
                lane_copy(l, j)
            for l, b, q, j in LAST:
                lane_store(l, "ffn", b, q, j)
            nc.scalar.activation(gap[:, 2:3], lift[:, 0:1], ACT.Sigmoid)
            act.wait_ge(bn_ready, 1)
            shift = bn_mv[:, 5:6]
            for s in range(WARM + LEN):
                for g in range(NG):
                    gs = slice(g * GC, (g + 1) * GC)
                    dst = state(s)[:, gs]
                    act.wait_ge(z_ready[g], s + 1)
                    nc.scalar.activation(dst, z_buf[:, gs], ACT.Sigmoid, bias=shift).then_inc(y_ready[g], 1)
            act.wait_ge(flag_ready, 1)
            far = act.value_load(flag[0:1, 0:1], min_val=0, max_val=1)
            DONE = WARM + LEN
            with act.If(far > 0):
                with act.Fori(0, SEQ) as k:
                    for s in range(LEN):
                        act.wait_ge(z_ready[0], DONE + k * LEN + s + 1)
                        nc.scalar.activation(seq_cols(ys, s, k + 1), z_buf[:, 0:B].rearrange("p (b o) -> p b o", o=1),
                                             ACT.Sigmoid, bias=shift).then_inc(y_ready[0], 1)

        @block.vector
        def _(dve):
            dve.sem_inc(lo_ready, 1)
            dve.sem_inc(o_normed, 1)
            dve.sem_inc(query_split, 2)
            dve.sem_inc(act_done, 1)
            dve.sem_inc(key_split, 1)
            steps = [0]

            def link(ins):
                ins.then_inc(dve_step, 1)
                steps[0] += 1
                dve.wait_ge(dve_step, steps[0])

            def rsqrt(src, v, y, w, after_each):
                after_each(nc.vector.tensor_scalar(v, src, 1e-5, None, ALU.add))
                after_each(nc.vector.tensor_scalar(w.bitcast(I32), v.bitcast(I32), 1, None, ALU.logical_shift_right))
                after_each(nc.vector.tensor_scalar(y.bitcast(I32), w.bitcast(I32), -1.0, GUESS, ALU.mult, ALU.add))
                for _ in range(3):
                    after_each(nc.vector.tensor_tensor(w, y, y, ALU.mult))
                    after_each(nc.vector.scalar_tensor_tensor(out=w, in0=w, scalar=-0.5, in1=v, op0=ALU.mult,
                                                              op1=ALU.mult))
                    after_each(nc.vector.scalar_tensor_tensor(out=y, in0=w, scalar=1.5, in1=y, op0=ALU.add,
                                                              op1=ALU.mult))

            def gn_count(b, q):
                nc.vector.bn_stats(gn_st[:, bass.ds(q, 1), :], X[:, cols(b, q)]).then_inc(gn_counted, 1)

            def gn_channels(b):
                dve.wait_ge(gn_counted, (b + 1) * NB)
                link(nc.vector.bn_aggr(gn_mv[:, :], gn_st[:, :, :].rearrange("p q s -> p (q s)")))
                mean, var = gn_mv[:, 0:1], gn_mv[:, 1:2]
                nc.vector.tensor_copy(gn_ms[:, 0:1], mean)
                link(nc.vector.tensor_tensor(gn_w[:, 2:3], mean, mean, ALU.mult))
                nc.vector.tensor_tensor(gn_ms[:, 1:2], var, gn_w[:, 2:3], ALU.add).then_inc(gn_sums, 1)

            def gn_scale(b):
                dve.wait_ge(gn_mean, b + 1)
                link(nc.vector.tensor_copy(gn_ms[:, :], small_bank[:, 0:2]))
                link(nc.vector.tensor_tensor(gn_w[:, 2:3], gn_ms[:, 0:1], gn_ms[:, 0:1], ALU.mult))
                link(nc.vector.tensor_tensor(gn_w[:, 0:1], gn_ms[:, 1:2], gn_w[:, 2:3], ALU.subtract))
                rsqrt(gn_w[:, 0:1], gn_w[:, 0:1], gn_w[:, 1:2], gn_w[:, 2:3], link)
                nc.vector.tensor_scalar(w_s[:, :, :].rearrange("p j c -> p (j c)"),
                                        w_t[:, 0:3, :].rearrange("p j c -> p (j c)"), gn_w[:, 1:2], None, ALU.mult)
                nc.vector.scalar_tensor_tensor(out=gn_w[:, 3:4], in0=gn_ms[:, 0:1], scalar=-1.0, in1=gn_w[:, 1:2],
                                               op0=ALU.mult, op1=ALU.mult).then_inc(gn_scaled, 1)

            def gn_bias(b):
                dve.wait_ge(gn_shift, b + 1)
                link(nc.vector.tensor_tensor(bias_s[:, 0:2], bias12[:, :], small_bank[:, 0:2], ALU.add))
                nc.vector.tensor_scalar(bias_s[:, 2:4], bias_s[:, 0:2], -1.0, None, ALU.mult)
                nc.vector.tensor_tensor(ba_s, ba_row[0:1, :], small_bank[0:1, 128:256], ALU.add) \
                    .then_inc(gn_done, 1)

            def prepare(b):
                s = b % 2
                if b:
                    done = ((b - 1) * NB + PAUSE) * 16
                    dve.wait_ge(sum_added, done + 1)
                    dve.wait_ge(lo_ready, done + 1)

                def split(q, h):
                    n = b * NB + q
                    dve.wait_ge(high_copied, n + 1)
                    nc.vector.scalar_tensor_tensor(out=key_a[s][CH:C, blk(q)], in0=prelu[h][1][CH:C, :],
                                                   scalar=bias_s[CH:C, 1:2], in1=hi_tmp[CH:C, :],
                                                   op0=ALU.add, op1=ALU.subtract).then_inc(key_split, 1)
                    nc.vector.scalar_tensor_tensor(out=query_b[s][0:CH, blk(q)], in0=prelu[h][0][0:CH, :],
                                                   scalar=bias_s[0:CH, 0:1], in1=query_a[s][0:CH, blk(q)],
                                                   op0=ALU.add, op1=ALU.subtract).then_inc(query_split, 1)

                def pair(i):
                    for h in range(2):
                        q = 2 * i + h
                        n = b * NB + q
                        dve.wait_ge(query_split, n + 1)
                        dve.wait_ge(value_split, n + 1)
                        dve.wait_ge(relu_done, n + 2)
                        for j in range(3):
                            last = nc.vector.scalar_tensor_tensor(out=prelu[h][j], in0=neg[h][j],
                                                                  scalar=one_less_a[:, j:j + 1],
                                                                  in1=proj_bank[3 * h + j], op0=ALU.mult, op1=ALU.add)
                        last.then_inc(act_done, 1)
                        if not isinstance(q, int) or q:
                            split(q - 1, 1 - h)

                pair(0)
                with dve.Fori(1, NB // 2) as i:
                    pair(i)
                split(NB - 1, 1)

            def reduce_max(b, ib, p, src=mx_bank):
                v = b * 128 + ib * 16 + p
                if p == 0:
                    dve.wait_ge(max_found, b * NB + ib)
                dve.wait_ge(mx_ready, v + 1)
                nc.vector.reduce_max(part_max[:, p:p + 1], src, AX.X).then_inc(mx_read, 1)

            def find_max(g):
                dve.wait_ge(mx_read, (g + 1) * 16)
                dve.wait_ge(max_turned, g)
                nc.vector.tensor_reduce(tile_max, part_max.rearrange("p (t k) -> p t k", k=4),
                                        AX.X, ALU.max).then_inc(max_found, 1)

            def split_max(g):
                dve.wait_ge(max_turned, g + 1)
                dve.wait_ge(m_moved, 32 * g)
                turned = small_bank[0:4, 0:128]
                nc.vector.tensor_scalar(m_hi, turned, -1.0 / MROW, None, ALU.mult).then_inc(m_hi_made, 1)
                dve.wait_ge(m_hi_made, g + 1)
                nc.vector.scalar_tensor_tensor(out=m_lo, in0=turned, scalar=-1.0 / MROW, in1=m_hi,
                                               op0=ALU.mult, op1=ALU.subtract).then_inc(m_ready, 1)

            dve.wait_ge(x_loaded[0], 16)
            for q in range(NB):
                gn_count(0, q)
            gn_channels(0)
            dve.wait_ge(w_ready, 1)
            gn_scale(0)
            gn_bias(0)
            dve.wait_ge(alpha_ready, 1)

            def invert(m, ib):
                dve.wait_ge(sums_ready, m * NB + ib + 1)
                nc.vector.reciprocal(inv_sum, small_bank[:, 0:4]).then_inc(inv_ready, 1)

            def split_inverse(m, ib):
                nb = m * NB + ib
                turned = small_bank[0:4, 0:128]
                dve.wait_ge(inv_turned, nb + 1)
                nc.vector.tensor_scalar(inv_hi, turned, INV, None, ALU.mult).then_inc(inv_hi_made, 1)
                dve.wait_ge(inv_hi_made, nb + 1)
                nc.vector.scalar_tensor_tensor(out=inv_lo, in0=turned, scalar=INV, in1=inv_hi,
                                               op0=ALU.mult, op1=ALU.subtract).then_inc(inv_split, 1)

            def normalise(m, ib):
                nb = m * NB + ib
                dve.wait_ge(inv_spread, nb + 1)
                dve.wait_ge(o_copied, nb + 1)
                dve.wait_ge(x_updated, nb)
                nc.vector.scalar_tensor_tensor(out=o_norm, in0=small_bank, scalar=1.0 / INV, in1=o_copy,
                                               op0=ALU.mult, op1=ALU.mult).then_inc(o_normed, 1)

            def invert_half(m, ib, half):
                nb = m * NB + ib
                hs = slice(half * HALF, (half + 1) * HALF)
                dve.wait_ge(sums_ready, nb + 1)
                dve.wait_ge(x_updated, nb)
                nc.vector.reciprocal(o_norm[:, hs], small_bank[:, hs]).then_inc(inv_made, 1)

            def weight(m, ib):
                nb = m * NB + ib
                dve.wait_ge(inv_made, 2 * (nb - B * NB) + 2)
                dve.wait_ge(o_copied, nb + 1)
                nc.vector.tensor_tensor(o_norm, o_norm, o_copy, ALU.mult).then_inc(o_normed, 1)

            def lane_stats(l, j, done):
                dve.wait_ge(lane_turned[l], j + 1)
                for t in range(4):
                    last = nc.vector.bn_stats(lane_st[:, 4 * l + t, :], bank(lane_bank[l])[:, t * 128:(t + 1) * 128])
                last.then_inc(lane_step[l], 1)
                dve.wait_ge(lane_step[l], done + 1)
                nc.vector.tensor_copy(lane_w[:, 2, 4 * l:4 * l + 4], lane_st[:, 4 * l:4 * l + 4, 1])
                for t in range(4):
                    last = nc.vector.bn_aggr(lane_mv[:, 4 * l + t, :], lane_st[:, 4 * l + t, :])
                last.then_inc(lane_step[l], 1)
                dve.wait_ge(lane_step[l], done + 2)

            def lane_rsqrt(l, j, k):
                mine = slice(4 * l, 4 * l + 4)
                v, y, w = [lane_w[:, i, mine] for i in range(3)]
                dve.wait_ge(lane_step[l], j * STEPS + 2 + k)
                if k == 0:
                    step = nc.vector.tensor_scalar(v, lane_mv[:, mine, 1], 1e-5, None, ALU.add)
                elif k == 1:
                    step = nc.vector.tensor_scalar(w.bitcast(I32), v.bitcast(I32), 1, None, ALU.logical_shift_right)
                elif k == 2:
                    step = nc.vector.tensor_scalar(y.bitcast(I32), w.bitcast(I32), -1.0, GUESS, ALU.mult, ALU.add)
                elif k % 3 == 0:
                    step = nc.vector.tensor_tensor(w, y, y, ALU.mult)
                elif k % 3 == 1:
                    step = nc.vector.scalar_tensor_tensor(out=w, in0=w, scalar=-0.5, in1=v, op0=ALU.mult,
                                                          op1=ALU.mult)
                else:
                    step = nc.vector.scalar_tensor_tensor(out=y, in0=w, scalar=1.5, in1=y, op0=ALU.add,
                                                          op1=ALU.mult)
                step.then_inc(lane_step[l], 1)

            def lane_shift(l):
                mine = slice(4 * l, 4 * l + 4)
                nc.vector.scalar_tensor_tensor(out=lane_w[:, 2, mine], in0=lane_mv[:, mine, 0], scalar=-1.0,
                                               in1=lane_w[:, 1, mine], op0=ALU.mult, op1=ALU.mult) \
                    .then_inc(rstd_ready[l], 1)

            def lane_count(l, b, q, j):
                dve.wait_ge(lane_stored[l], j + 1)
                nc.vector.bn_stats(bn_st[:, bass.ds(b * NB + q, 1), :], wx[:, wx_cols(b, q)]).then_inc(wx_counted, 1)

            def attend(m, follows):
                def body(ib):
                    has_before = follows or not isinstance(ib, int) or ib > 0
                    chained = m < B - 1 or m == B - 1 and not (isinstance(ib, int) and ib == NB - 1)
                    norms_next = m + 1 < B and isinstance(ib, int) and ib == PAUSE - 1
                    for p in range(NP):
                        n = m * 128 + ib * 16 + p
                        unit = max_unit(m, ib, p)
                        steps = [(l, j, 4 * (p - 2 - 7 * l)) for l, kind, b, q, j in jobs(m, ib)
                                 if p in range(2 + 7 * l, 5 + 7 * l)]
                        for l, j, k in steps:
                            lane_rsqrt(l, j, k)
                        if unit:
                            reduce_max(*unit)
                        for l, j, k in steps:
                            lane_rsqrt(l, j, k + 1)
                        if p == 7 and chained:
                            find_max(m * NB + ib + 1)
                        if m + 1 < B and isinstance(ib, int) and ib == PAUSE and p == 0:
                            dve.wait_ge(key_split, (m + 2) * NB + 1)
                            dve.wait_ge(query_split, (m + 2) * NB + 2)
                            dve.wait_ge(value_split, (m + 2) * NB + 2)
                        dve.wait_ge(full_ready, n + 2)
                        dve.wait_ge(pv_done, n + 2)
                        nc.vector.tensor_tensor(p_lo[p % 2], p_full[p % 2], p_hi[p % 4], ALU.subtract) \
                            .then_inc(lo_ready, 1)
                        if has_before:
                            pm, pb = before(m, ib)
                            if pm < B:
                                if p == after(m):
                                    invert(pm, pb)
                                if p == after(m) + 2:
                                    split_inverse(pm, pb)
                                if p == after(m) + 4:
                                    normalise(pm, pb)
                            else:
                                if p in (after(m), after(m) + 1):
                                    invert_half(pm, pb, p - after(m))
                                if p == after(m) + 2:
                                    weight(pm, pb)
                        for l, kind, b, q, j in jobs(m, ib):
                            if p == 1 + 7 * l:
                                lane_stats(l, j, j * STEPS)
                            if p in range(2 + 7 * l, 5 + 7 * l):
                                lane_rsqrt(l, j, 4 * (p - 2 - 7 * l) + 2)
                                lane_rsqrt(l, j, 4 * (p - 2 - 7 * l) + 3)
                            if p == 4 + 7 * l:
                                dve.wait_ge(lane_step[l], (j + 1) * STEPS)
                                lane_shift(l)
                            if p == 15 and kind == "ffn":
                                lane_count(l, b, q, j)
                        if p == 13 and chained:
                            split_max(m * NB + ib + 1)
                        if isinstance(ib, int) and ib == 0 and m + 1 < B and p in (1, 4, 8, 11):
                            if p == 1:
                                dve.wait_ge(x_loaded[m + 1], 16)
                            gn_count(m + 1, (1, 4, 8, 11).index(p))
                        if not isinstance(ib, int) and m + 1 < B and p == 11:
                            gn_count(m + 1, NB // 2 - 1 + ib)
                        if norms_next:
                            if p == 1:
                                gn_channels(m + 1)
                            if p == 2:
                                gn_scale(m + 1)
                            if p == NP - 1:
                                gn_bias(m + 1)

                body(0)
                if m < B:
                    with dve.Fori(1, PAUSE - 1) as ib:
                        body(ib)
                    body(PAUSE - 1)
                    if m + 1 < B:
                        prepare(m + 1)
                    body(PAUSE)
                    body(PAUSE + 1)
                else:
                    first = LAG if m == 2 * B - 1 else 1
                    for ib in range(1, first):
                        body(ib)
                    with dve.Fori(first, NB) as ib:
                        body(ib)

            def finish(m):
                invert_half(m, NB - 1, 0)
                invert_half(m, NB - 1, 1)
                weight(m, NB - 1)

            prepare(0)
            for v in range(LEAD):
                if v == 16:
                    find_max(0)
                reduce_max(0, v // 16, v % 16, lead_bank(v))
                if v == 17:
                    split_max(0)
            for m in range(2 * B):
                attend(m, follows=m > 0)
            finish(2 * B - 1)
            for l, b, q, j in LAST:
                lane_stats(l, j, j * STEPS)
            link(nc.vector.tensor_copy(lane_w[:, 0, :], lane_mv[:, :, 1]))
            rsqrt(lane_w[:, 0, :], lane_w[:, 0, :], lane_w[:, 1, :], lane_w[:, 2, :], link)
            for l, b, q, j in LAST:
                lane_shift(l)
            for l, b, q, j in LAST:
                dve.wait_ge(lane_done[l], j + 1)
            link(nc.vector.memset(z_buf, 0.0))
            for l, b, q, j in LAST:
                lane_count(l, b, q, j)

            dve.wait_ge(wx_counted, B * NB)
            link(nc.vector.bn_aggr(bn_mv[:, 0:2], bn_st[:, :, :].rearrange("p j s -> p (j s)")))
            rsqrt(bn_mv[:, 1:2], bn_mv[:, 7:8], bn_mv[:, 3:4], bn_mv[:, 8:9], link)
            link(nc.vector.tensor_tensor(bn_mv[:, 4:5], bn_mv[:, 3:4], gb[:, 0:1], ALU.mult))
            link(nc.vector.tensor_tensor(bn_mv[:, 6:7], bn_mv[:, 0:1], bn_mv[:, 4:5], ALU.mult))
            nc.vector.tensor_tensor(bn_mv[:, 5:6], gb[:, 1:2], bn_mv[:, 6:7], ALU.subtract).then_inc(bn_ready, 1)
            dve.wait_ge(bn_ready, 1)
            gain = bn_mv[:, 4:5]

            def batch_cols(g, s):
                if s >= WARM:
                    return wx_steps[:, g * GC:(g + 1) * GC, s - WARM], 0
                return wx_steps[:, g * GC:(g + 1) * GC - 1, LEN - WARM + s], 1

            for s in range(WARM + LEN):
                for g in range(NG):
                    src, skip = batch_cols(g, s)
                    z = z_buf[:, g * GC + skip:(g + 1) * GC]
                    if s == 0:
                        nc.vector.tensor_scalar(z, src, gain, None, ALU.mult).then_inc(z_ready[g], 1)
                    else:
                        dve.wait_ge(vy_ready[g], s)
                        nc.vector.scalar_tensor_tensor(out=z, in0=src, scalar=gain,
                                                       in1=bank(g)[:, skip:GC], op0=ALU.mult,
                                                       op1=ALU.add).then_inc(z_ready[g], 1)
                if s == WARM - 1:
                    for g in range(NG):
                        dve.wait_ge(y_ready[g], WARM)
                    nc.vector.memset(y_began.rearrange("p (b k) -> p b k", b=B)[:, :, 0:1], 0.0) \
                        .then_inc(start_set, 1)
            for g in range(NG):
                dve.wait_ge(y_ready[g], WARM + LEN)
            dve.wait_ge(start_set, 1)
            began = y_began.rearrange("p (b k) -> p b k", b=B)[:, :, 1:CHUNKS]
            ended = ys[:, LEN - 1, :].rearrange("p (b k) -> p b k", b=B)[:, :, 0:CHUNKS - 1]
            diff = z_buf[:, 0:B * (CHUNKS - 1)].rearrange("p (b k) -> p b k", b=B)
            link(nc.vector.tensor_tensor(diff, began, ended, ALU.subtract))
            link(nc.vector.tensor_tensor(diff, diff, diff, ALU.mult))
            link(nc.vector.tensor_scalar(diff, diff, CLOSE * CLOSE, None, ALU.is_le))
            nc.vector.tensor_reduce(gap[:, 0:1], diff, AX.XY, ALU.min).then_inc(gap_ready, 1)
            dve.wait_ge(gap_max, 1)
            link(nc.vector.tensor_reduce(gap[0:1, 1:2], small_bank[0:1, 0:128], AX.X, ALU.min))
            nc.vector.tensor_scalar(flag[0:1, 0:1], gap[0:1, 1:2], -1.0, 1.0, ALU.mult, ALU.add) \
                .then_inc(flag_ready, 1)
            dve.wait_ge(flag_ready, 1)
            far = dve.value_load(flag[0:1, 0:1], min_val=0, max_val=1)
            DONE = WARM + LEN
            with dve.If(far > 0):
                with dve.Fori(0, SEQ) as k:
                    for s in range(LEN):
                        dve.wait_ge(vy_ready[0], DONE - 1 + k * LEN + s + 1)
                        src = wx_steps[:, :, s].rearrange("p (b k) -> p b k", b=B)[:, :, bass.ds(k + 1, 1)]
                        nc.vector.scalar_tensor_tensor(
                            out=z_buf[:, 0:B].rearrange("p (b o) -> p b o", o=1), in0=src, scalar=gain,
                            in1=bank(0)[:, 0:B].rearrange("p (b o) -> p b o", o=1),
                            op0=ALU.mult, op1=ALU.add).then_inc(z_ready[0], 1)
                dve.wait_ge(y_ready[0], DONE + SEQ * LEN)
            dve.sem_inc(states_final, 1)
            for b in range(B - 1):
                for half in range(2):
                    x_b, y_b = last_sum(b, half)
                    nc.vector.tensor_tensor(x_b, x_b, y_b, ALU.add).then_inc(out_ready, 1)

        @block.gpsimd
        def _(pool):
            pool.sem_inc(sum_added, 1)
            pool.sem_inc(value_split, 2)
            made = [0]

            def link(ins):
                ins.then_inc(pool_step, 1)
                made[0] += 1
                pool.wait_ge(pool_step, made[0])

            nc.gpsimd.memset(ones[:, :], 1.0)
            nc.gpsimd.memset(zero[:, :], 0.0)
            nc.gpsimd.memset(lift[:, 0:1], LIFT)
            nc.gpsimd.memset(lift[:, 1:2], LIFT - ROWMAX)
            nc.gpsimd.memset(ident[:, :], 0.0)
            link(nc.gpsimd.memset(group_mean[:, :], 1.0 / GROUP))
            for s in range(2):
                link(nc.gpsimd.memset(key_b[s][CH:CH + 2, :], MROW))
            nc.gpsimd.affine_select(out=ident[:, :], in_=ident[:, :], compare_op=ALU.not_equal, fill=1.0,
                                    base=0, pattern=[[-1, C]], channel_multiplier=1)
            gm = group_mean[:, :].rearrange("p (g r) -> p g r", r=GROUP)
            link(nc.gpsimd.affine_select(out=gm, in_=gm, compare_op=ALU.is_ge, fill=0.0, base=0,
                                         pattern=[[-GROUP, C // GROUP], [0, GROUP]], channel_multiplier=1))
            link(nc.gpsimd.affine_select(out=gm, in_=gm, compare_op=ALU.is_ge, fill=0.0, base=GROUP - 1,
                                         pattern=[[GROUP, C // GROUP], [0, GROUP]], channel_multiplier=-1))
            nc.gpsimd.tensor_copy(ident16[:, :], ident[:, :]).then_inc(consts_set, 1)

            def zeros(rows, n):
                return zero[0:rows, 0:1].broadcast_to([rows, n])

            def prepare(b):
                s = b % 2
                with pool.Fori(0, NB // 2) as i:
                    for h in range(2):
                        n = b * NB + 2 * i + h
                        q = blk(2 * i + h)
                        pool.wait_ge(act_done, n + 2)
                        nc.gpsimd.tensor_tensor(value_hi[s][:, q], prelu[h][2], zeros(C, BLK), ALU.add) \
                            .then_inc(value_copied, 1)
                        nc.gpsimd.tensor_tensor(key_b[s][0:CH, q], prelu[h][1][0:CH, :],
                                                bias_s[0:CH, 1:2].broadcast_to([CH, BLK]), ALU.add)
                        pool.wait_ge(value_copied, n + 1)
                        nc.gpsimd.tensor_tensor(value_lo[s][:, q], prelu[h][2], value_hi[s][:, q], ALU.subtract) \
                            .then_inc(value_split, 1)

            def lane_lo(l, b, q, j):
                pool.wait_ge(t_hi_ready, j + 1)
                nc.gpsimd.tensor_tensor(t_lo[b % 2][:, blk(q)], lane_t[l], t_hi[b % 2][:, blk(q)], ALU.subtract) \
                    .then_inc(t_lo_ready, 1)

            def update(m, ib):
                nb = m * NB + ib
                pool.wait_ge(o_normed, nb + 2)
                x_b = X[:, cols(m % B, ib)]
                nc.gpsimd.tensor_tensor(x_b, x_b, o_norm, ALU.add).then_inc(x_updated, 1)

            def attend(m, follows):
                def body(ib):
                    has_before = follows or not isinstance(ib, int) or ib > 0
                    for p in range(NP):
                        nb = m * NB + ib
                        n = nb * 16 + p
                        full = p_full[p % 2]
                        pool.wait_ge(full_ready, n + 2)
                        pool.wait_ge(sum_added, n + 1)
                        if p == 0:
                            pool.wait_ge(sums_folded, nb)
                        if p == 0:
                            last = nc.gpsimd.tensor_tensor(sum_run, full, zeros(C, 1024), ALU.add)
                        else:
                            last = nc.gpsimd.tensor_tensor(sum_run, sum_run, full, ALU.add)
                        last.then_inc(sum_added, 1)
                        if p == NP - 1:
                            pool.wait_ge(sum_added, n + 2)
                            pool.wait_ge(sums_ready, nb)
                            nc.gpsimd.tensor_tensor(sum_end, sum_run[:, 0:BLK], sum_run[:, BLK:2 * BLK], ALU.add) \
                                .then_inc(sums_folded, 1)
                        for l, kind, b, q, j in jobs(m, ib):
                            if p == 7 and kind == "tokens":
                                lane_lo(l, b, q, j)
                        if p == after(m) + 5 and has_before:
                            update(*before(m, ib))

                body(0)
                if m < B:
                    with pool.Fori(1, PAUSE - 1) as ib:
                        body(ib)
                    body(PAUSE - 1)
                    if m + 1 < B:
                        prepare(m + 1)
                    body(PAUSE)
                    body(PAUSE + 1)
                else:
                    with pool.Fori(1, NB) as ib:
                        body(ib)

            prepare(0)
            for m in range(2 * B):
                attend(m, follows=m > 0)
            update(2 * B - 1, NB - 1)
            pool.wait_ge(states_final, 1)
            for half in range(2):
                x_b, y_b = last_sum(B - 1, half)
                nc.gpsimd.tensor_tensor(x_b, x_b, y_b, ALU.add).then_inc(last_ready, 1)


_INS = ['x', 'L0_conv_w1', 'L0_conv_b1', 'L0_conv_a1', 'L0_conv_w2', 'L0_conv_b2', 'L0_conv_a2', 'L0_conv_wa',
        'L0_conv_ba', 'L0_conv_aa', 'L1_ffn_W', 'L1_ffn_V', 'L1_ffn_gamma', 'L1_ffn_beta']


def kernel(**inputs):
    import numpy as _np
    import concourse.bacc as _bacc
    from concourse import mybir as _mybir
    from concourse.bass_utils import run_bass_kernel_spmd as _run

    nc = _bacc.Bacc("TRN2", target_bir_lowering=False, num_devices=1)
    n, c, h, w = inputs["x"].shape
    shapes = {"x": (n, c, h * w), "L0_conv_ba": (1, c)}
    arrays, args = {}, []
    for name in _INS:
        a = _np.ascontiguousarray(inputs[name])
        if name in shapes:
            a = a.reshape(shapes[name])
        elif a.ndim < 2:
            a = a.reshape(-1, 1)
        arrays[f"in_{name}"] = a
        args.append(nc.dram_tensor(f"in_{name}", a.shape, _mybir.dt.from_np(a.dtype), kind="ExternalInput").ap())
    args.append(nc.dram_tensor("out_0", (n, c, h * w), _mybir.dt.float32, kind="ExternalOutput").ap())
    hybrid_kernel(nc, *args)
    r = _run(nc, [arrays], core_ids=[0])
    return r.results[0]["out_0"].reshape(n, c, h, w)
```
